# Optimizing a Trainium2 kernel written in Bass

```python
import numpy as np
import jax
import jax.numpy as jnp

def _softmax(x, axis=-1):
    return jax.nn.softmax(x, axis=axis)

def _gelu(x):
    return jax.nn.gelu(x, approximate=True)

def _silu(x):
    return jax.nn.silu(x)

def _sigmoid(x):
    return jax.nn.sigmoid(x)

def _layernorm(x, axis=-1, eps=1e-05):
    m = jnp.mean(x, axis=axis, keepdims=True)
    v = jnp.var(x, axis=axis, keepdims=True)
    return (x - m) / jnp.sqrt(v + eps)

def _scatter_add(tgt, idx, src, axis=0):
    return tgt.at[idx].add(src)

def _segment_sum(src, seg, n):
    return jax.ops.segment_sum(src, seg, n)
kernel_name = 'mk_metaformer_d1_conv_nhwc512_r4_652646'

def setup_inputs(seed: int=0):
    np.random.seed(seed)
    _w = jnp.asarray

    def _rec_inputs():
        import jax
        import jax.numpy as jnp
        _gk = jax.random.key(seed)
        x = -0.000125 + 0.9999 * jax.random.normal(jax.random.fold_in(_gk, 1), (1, 32, 128, 128), jnp.float32)
        return x
    x = _rec_inputs()

    def _L0_conv_setup():
        import jax, jax.numpy as jnp
        import numpy as np
        DZ = 32
        DC = 32
        B, L = (1, 128)

        def _ln(x, w, b, eps=1e-05):
            mu = jnp.mean(x, axis=-1, keepdims=True)
            var = jnp.mean(jnp.square(x - mu), axis=-1, keepdims=True)
            return (x - mu) * jax.lax.rsqrt(var + eps) * w + b

        def _lin(x, w, b):
            return x @ w + b
        key = jax.random.key(seed)
        ks = jax.random.split(key, 32)
        s_z = 1.0 / np.sqrt(DZ)
        s_c = 1.0 / np.sqrt(DC)
        d = {'z1': jax.random.normal(ks[0], (B, DZ, L, L), jnp.float32), 'z2': jax.random.normal(ks[1], (B, DZ, L, L), jnp.float32), 'z3': jax.random.normal(ks[2], (B, DZ, L, L), jnp.float32), 'ln1_w': jnp.ones((DZ,), jnp.float32), 'ln1_b': jnp.zeros((DZ,), jnp.float32), 'ln2_w': jnp.ones((DZ,), jnp.float32), 'ln2_b': jnp.zeros((DZ,), jnp.float32), 'ln3_w': jnp.ones((DZ,), jnp.float32), 'ln3_b': jnp.zeros((DZ,), jnp.float32), 'ln5_w': jnp.ones((DC,), jnp.float32), 'ln5_b': jnp.zeros((DC,), jnp.float32)}
        names = ['l1', 'l2', 'l3', 'l4', 'g1', 'g2', 'g3', 'g4']
        for i, n in enumerate(names):
            d[n + '_w'] = jax.random.normal(ks[3 + i], (DZ, DC), jnp.float32) * s_z
            d[n + '_b'] = jnp.zeros((DC,), jnp.float32)
        d['l5_w'] = jax.random.normal(ks[11], (DC, DZ), jnp.float32) * s_c
        d['l5_b'] = jnp.zeros((DZ,), jnp.float32)
        d['g5_w'] = jax.random.normal(ks[12], (DC, DZ), jnp.float32) * s_c
        d['g5_b'] = jnp.zeros((DZ,), jnp.float32)
        return d
    _L0_conv_all = _L0_conv_setup()
    _L0_conv_in = {k: v for k, v in _L0_conv_all.items() if k in ('z2', 'z3', 'ln1_w', 'ln1_b', 'ln2_w', 'ln2_b', 'ln3_w', 'ln3_b', 'ln5_w', 'ln5_b', 'l1_w', 'l1_b', 'l2_w', 'l2_b', 'l3_w', 'l3_b', 'l4_w', 'l4_b', 'l5_w', 'l5_b', 'g1_w', 'g1_b', 'g2_w', 'g2_b', 'g3_w', 'g3_b', 'g4_w', 'g4_b', 'g5_w', 'g5_b')}
    del _L0_conv_all

    def _L0_ffn_setup():
        import jax, jax.numpy as jnp
        import numpy as np
        B, S, H, E, K = (8, 512, 128, 8, 2)
        key = jax.random.key(seed)
        ks = jax.random.split(key, 6)
        scale = 1.0 / np.sqrt(H)
        return {'x': jax.random.normal(ks[0], (B, S, H), dtype=jnp.float32), 'W_g': jax.random.normal(ks[1], (H, E), dtype=jnp.float32) * scale, 'w1': jax.random.normal(ks[2], (E, H, 4 * H), dtype=jnp.float32) * scale, 'b1': jnp.zeros((E, 4 * H), dtype=jnp.float32), 'w2': jax.random.normal(ks[3], (E, 4 * H, H), dtype=jnp.float32) * (1.0 / np.sqrt(4 * H)), 'b2': jnp.zeros((E, H), dtype=jnp.float32)}
    _L0_ffn_all = _L0_ffn_setup()
    _L0_ffn_in = {k: v for k, v in _L0_ffn_all.items() if k in ('W_g', 'w1', 'b1', 'w2', 'b2')}
    del _L0_ffn_all
    return {'x': x, 'L0_conv_z2': _L0_conv_in['z2'], 'L0_conv_z3': _L0_conv_in['z3'], 'L0_conv_ln1_w': _L0_conv_in['ln1_w'], 'L0_conv_ln1_b': _L0_conv_in['ln1_b'], 'L0_conv_ln2_w': _L0_conv_in['ln2_w'], 'L0_conv_ln2_b': _L0_conv_in['ln2_b'], 'L0_conv_ln3_w': _L0_conv_in['ln3_w'], 'L0_conv_ln3_b': _L0_conv_in['ln3_b'], 'L0_conv_ln5_w': _L0_conv_in['ln5_w'], 'L0_conv_ln5_b': _L0_conv_in['ln5_b'], 'L0_conv_l1_w': _L0_conv_in['l1_w'], 'L0_conv_l1_b': _L0_conv_in['l1_b'], 'L0_conv_l2_w': _L0_conv_in['l2_w'], 'L0_conv_l2_b': _L0_conv_in['l2_b'], 'L0_conv_l3_w': _L0_conv_in['l3_w'], 'L0_conv_l3_b': _L0_conv_in['l3_b'], 'L0_conv_l4_w': _L0_conv_in['l4_w'], 'L0_conv_l4_b': _L0_conv_in['l4_b'], 'L0_conv_l5_w': _L0_conv_in['l5_w'], 'L0_conv_l5_b': _L0_conv_in['l5_b'], 'L0_conv_g1_w': _L0_conv_in['g1_w'], 'L0_conv_g1_b': _L0_conv_in['g1_b'], 'L0_conv_g2_w': _L0_conv_in['g2_w'], 'L0_conv_g2_b': _L0_conv_in['g2_b'], 'L0_conv_g3_w': _L0_conv_in['g3_w'], 'L0_conv_g3_b': _L0_conv_in['g3_b'], 'L0_conv_g4_w': _L0_conv_in['g4_w'], 'L0_conv_g4_b': _L0_conv_in['g4_b'], 'L0_conv_g5_w': _L0_conv_in['g5_w'], 'L0_conv_g5_b': _L0_conv_in['g5_b'], 'L0_ffn_W_g': _L0_ffn_in['W_g'], 'L0_ffn_w1': _L0_ffn_in['w1'], 'L0_ffn_b1': _L0_ffn_in['b1'], 'L0_ffn_w2': _L0_ffn_in['w2'], 'L0_ffn_b2': _L0_ffn_in['b2']}

def reference(x, L0_conv_z2, L0_conv_z3, L0_conv_ln1_w, L0_conv_ln1_b, L0_conv_ln2_w, L0_conv_ln2_b, L0_conv_ln3_w, L0_conv_ln3_b, L0_conv_ln5_w, L0_conv_ln5_b, L0_conv_l1_w, L0_conv_l1_b, L0_conv_l2_w, L0_conv_l2_b, L0_conv_l3_w, L0_conv_l3_b, L0_conv_l4_w, L0_conv_l4_b, L0_conv_l5_w, L0_conv_l5_b, L0_conv_g1_w, L0_conv_g1_b, L0_conv_g2_w, L0_conv_g2_b, L0_conv_g3_w, L0_conv_g3_b, L0_conv_g4_w, L0_conv_g4_b, L0_conv_g5_w, L0_conv_g5_b, L0_ffn_W_g, L0_ffn_w1, L0_ffn_b1, L0_ffn_w2, L0_ffn_b2):
    import jax
    import jax.numpy as jnp

    def _L0_conv_ref(z1, z2, z3, ln1_w, ln1_b, ln2_w, ln2_b, ln3_w, ln3_b, ln5_w, ln5_b, l1_w, l1_b, l2_w, l2_b, l3_w, l3_b, l4_w, l4_b, l5_w, l5_b, g1_w, g1_b, g2_w, g2_b, g3_w, g3_b, g4_w, g4_b, g5_w, g5_b):
        import jax, jax.numpy as jnp
        import numpy as np
        DZ = 32
        DC = 32
        B, L = (1, 128)

        def _ln(x, w, b, eps=1e-05):
            mu = jnp.mean(x, axis=-1, keepdims=True)
            var = jnp.mean(jnp.square(x - mu), axis=-1, keepdims=True)
            return (x - mu) * jax.lax.rsqrt(var + eps) * w + b

        def _lin(x, w, b):
            return x @ w + b
        a = _ln(jnp.transpose(z1, (0, 2, 3, 1)), ln1_w, ln1_b)
        b_ = _ln(jnp.transpose(z2, (0, 2, 3, 1)), ln2_w, ln2_b)
        c = _ln(jnp.transpose(z3, (0, 2, 3, 1)), ln3_w, ln3_b)
        r = a
        z12 = _lin(a, l1_w, l1_b) * jax.nn.sigmoid(_lin(a, g1_w, g1_b))
        z13 = _lin(a, l2_w, l2_b) * jax.nn.sigmoid(_lin(a, g2_w, g2_b))
        p2 = _lin(b_, l3_w, l3_b) * jax.nn.sigmoid(_lin(b_, g3_w, g3_b))
        p3 = _lin(c, l4_w, l4_b) * jax.nn.sigmoid(_lin(c, g4_w, g4_b))
        t1 = jnp.einsum('bikc,bkjc->bijc', p2, z12)
        t2 = jnp.einsum('bikc,bjkc->bjic', p3, z13)
        z = t1 + t2
        z = jax.nn.sigmoid(_lin(r, g5_w, g5_b)) * _lin(_ln(z, ln5_w, ln5_b), l5_w, l5_b)
        z = jax.nn.elu(z)
        return jnp.transpose(z, (0, 3, 1, 2))

    def _L0_ffn_ref(x, W_g, w1, b1, w2, b2):
        import jax, jax.numpy as jnp
        import numpy as np
        B, S, H, E, K = (8, 512, 128, 8, 2)
        logits = jnp.einsum('bsh,he->bse', jax.lax.stop_gradient(x), W_g)
        probs = jax.nn.softmax(logits, axis=-1)
        top_w, top_idx = jax.lax.top_k(probs, K)
        h = jnp.einsum('bsh,ehf->bsef', x, w1) + b1
        h = jax.nn.gelu(h, approximate=False)
        expert_out = jnp.einsum('bsef,efh->bseh', h, w2) + b2
        sel = jnp.take_along_axis(expert_out, top_idx[..., None], axis=2)
        out = jnp.einsum('bskh,bsk->bsh', sel, top_w)
        return out

    def _gn(v, G=32, eps=1e-05):
        B_, H_, W_, C_ = v.shape
        g = v.reshape(B_, H_, W_, G, C_ // G)
        m = jnp.mean(g, axis=(1, 2, 4), keepdims=True)
        s = jnp.var(g, axis=(1, 2, 4), keepdims=True)
        return ((g - m) / jnp.sqrt(s + eps)).reshape(v.shape)

    def _ln_c(v, eps=1e-06):
        m = jnp.mean(v, axis=-1, keepdims=True)
        s = jnp.var(v, axis=-1, keepdims=True)
        return (v - m) / jnp.sqrt(s + eps)

    def _ln_t(v, eps=1e-05):
        m = jnp.mean(v, axis=-1, keepdims=True)
        s = jnp.var(v, axis=-1, keepdims=True)
        return (v - m) / jnp.sqrt(s + eps)

    def _to_tokens(v):
        B_, H_, W_, C_ = v.shape
        return v.reshape(B_, H_ * W_, C_)

    def _from_tokens(t, like):
        return t.reshape(like.shape)
    x = x + _L0_conv_ref(_ln_c(x), L0_conv_z2, L0_conv_z3, L0_conv_ln1_w, L0_conv_ln1_b, L0_conv_ln2_w, L0_conv_ln2_b, L0_conv_ln3_w, L0_conv_ln3_b, L0_conv_ln5_w, L0_conv_ln5_b, L0_conv_l1_w, L0_conv_l1_b, L0_conv_l2_w, L0_conv_l2_b, L0_conv_l3_w, L0_conv_l3_b, L0_conv_l4_w, L0_conv_l4_b, L0_conv_l5_w, L0_conv_l5_b, L0_conv_g1_w, L0_conv_g1_b, L0_conv_g2_w, L0_conv_g2_b, L0_conv_g3_w, L0_conv_g3_b, L0_conv_g4_w, L0_conv_g4_b, L0_conv_g5_w, L0_conv_g5_b)
    t = _to_tokens(x)
    t = t + _L0_ffn_ref(_ln_t(t), L0_ffn_W_g, L0_ffn_w1, L0_ffn_b1, L0_ffn_w2, L0_ffn_b2)
    x = _from_tokens(t, x)
    return x

_drawn_inputs = setup_inputs


def setup_inputs(seed=0):
    import zlib

    import numpy as np

    out = dict(_drawn_inputs(seed))
    spreads = {'L0_conv_ln1_w': (1.0, 0.2),
     'L0_conv_ln1_b': (0.0, 0.1),
     'L0_conv_ln2_w': (1.0, 0.2),
     'L0_conv_ln2_b': (0.0, 0.1),
     'L0_conv_ln3_w': (1.0, 0.2),
     'L0_conv_ln3_b': (0.0, 0.1),
     'L0_conv_ln5_w': (1.0, 0.2),
     'L0_conv_ln5_b': (0.0, 0.1),
     'L0_conv_l1_b': (0.0, 0.1),
     'L0_conv_l2_b': (0.0, 0.1),
     'L0_conv_l3_b': (0.0, 0.1),
     'L0_conv_l4_b': (0.0, 0.1),
     'L0_conv_l5_b': (0.0, 0.1),
     'L0_conv_g1_b': (0.0, 0.387),
     'L0_conv_g2_b': (0.0, 0.441),
     'L0_conv_g3_b': (0.0, 0.406),
     'L0_conv_g4_b': (0.0, 0.519),
     'L0_conv_g5_b': (0.0, 0.385),
     'L0_ffn_b1': (0.0, 0.304),
     'L0_ffn_b2': (0.0, 0.1)}
    factors = {}
    for name, (base, spread) in spreads.items():
        noise = np.random.default_rng([zlib.crc32(name.encode()), seed]).standard_normal(out[name].shape)
        drawn = base * np.exp(spread * noise) if base else spread * noise
        out[name] = jnp.asarray(drawn.astype(out[name].dtype))
    for name, factor in factors.items():
        out[name] = (out[name] * factor).astype(out[name].dtype)
    return out
```

```python
from contextlib import ExitStack

import concourse.bass as bass
from concourse import mybir

ALU = mybir.AluOpType
ACT = mybir.ActivationFunctionType
F32 = mybir.dt.float32
BF16 = mybir.dt.bfloat16
I32 = mybir.dt.int32
AX = mybir.AxisListType

P = 128
C = 32
Q = P // C
CH = P // Q
NCH = 4
SLOTS = 10
GROUPS = [(0, 5), (5, 7), (7, 9), (9, 10)]
E_ = 8
F = 512
TOP = 2
TILES = 72
RING = 4
EPS_C, EPS = 1e-6, 1e-5


def build(nc, x, z2, z3, conv_w, conv_b, ln_p, W_g, w1, b1, w2, b2, out):
    with ExitStack() as ctx:
        def sb(name, shape, dt=F32):
            return ctx.enter_context(nc.sbuf_tensor(name, shape, dt))

        def sem(name):
            return ctx.enter_context(nc.semaphore(name))

        bank = [ctx.enter_context(nc.psum_tensor(f"bank{i}", [P, 512], F32)) for i in range(8)]

        X = sb("X", [P, C, P])
        Z23 = sb("Z23", [P, 2, C, P])
        Z2, Z3 = Z23[:, 0], Z23[:, 1]
        ZA = sb("ZA", [P, C, P])
        ZB = sb("ZB", [P, C, P])
        ZD = sb("ZD", [P, P, C])
        p2T = sb("p2T", [P, C, P])
        p3T = sb("p3T", [P, C, P])
        z12, z13 = Z2, Z3
        R = sb("R", [P, SLOTS, Q, C])
        RS = sb("RS", [P, SLOTS, Q, C])
        lnp = sb("lnp", [P, 4, 2])
        lnb = sb("lnb", [P, 4, 96])
        braw = sb("braw", [96, SLOTS, C])
        ZDf = ZD[:].rearrange("p a b -> p (a b)")
        bsum = ZDf[0:96, 0:SLOTS * P].rearrange("p (s q c) -> p s q c", s=SLOTS, q=Q)
        bhi = ZDf[0:96, 2048:2048 + SLOTS * C * 2].bitcast(BF16)
        bmid = ZDf[0:96, 3072:3072 + SLOTS * C * 2].bitcast(BF16)
        BB = sb("BB", [96, SLOTS * P], BF16)
        pick3 = sb("pick3", [96, P], BF16)
        ident = sb("ident", [P, P])
        blk = sb("blk", [P, P])
        cen = sb("cen", [P, P])
        mhalf = sb("mhalf", [P, C])
        sq = sb("sq", [P, 2, 512])
        sd = sb("sd", [P, 2, 512])
        rn = sb("rn", [P, 2, 512])
        sg = sb("sg", [P, 2, 256])
        epsc = sb("epsc", [P, 1])
        bn = sb("bn", [P, C, 6])
        st = sb("st", [P, 8, C])
        mu = sb("mu", [P, P])
        var = sb("var", [P, P])
        rsd = sb("rsd", [P, P])
        um, ue = sq, sd

        Asq = ctx.enter_context(nc.sbuf_tensor("Asq", [P, CH * C], F32))
        sig5 = ZA[:].rearrange("p a b -> p (a b)").rearrange("p (j c) -> p j c", c=C)
        Zt = ZB
        p3j = p3T[:].rearrange("p a b -> p (a b)").rearrange("p (j c) -> p j c", c=C)
        T5 = p2T

        w1s = Z2.rearrange("p c j -> p (c j)")
        w2s = Z3.rearrange("p c j -> p (c j)")
        b1s = ZD[:].rearrange("p a b -> p (a b)")
        b2s = sb("b2s", [P, E_ * P])
        XL = ZB
        XT = p2T
        BH = p3T[:].rearrange("p a b -> p (a b)").bitcast(BF16).rearrange("p (n b) -> p n b", b=P)
        AW = sb("AW", [P, TOP * C, 2, TILES], BF16)
        wg = sb("wg", [P, E_])
        ZAf = ZA[:].rearrange("p a b -> p (a b)")
        rt = ZAf[:, 0:12 * C * E_].rearrange("p (k n) -> p k n", k=12)
        te = ZAf[:, 12 * C * E_:12 * C * E_ + TILES * E_].rearrange("p (t e) -> p t e", e=E_)
        rs_ = sb("rs_", [P, 10, C])
        re_ = sb("re_", [P, 8, E_])
        prob = sb("prob", [P, TOP, C])
        slot = sb("slot", [P, TOP, C])
        sloti = sb("sloti", [P, 3, TOP * C], I32)
        slota = sb("slota", [P, 2, TOP * C])
        M_ = sb("M_", [P, C * E_], BF16)
        lower = sb("lower", [P, P], BF16)
        ones = sb("ones", [P, P], BF16)
        iota_w = sb("iota_w", [P, P])
        iota_p = sb("iota_p", [P, 1])
        spare = sb("spare", [P, TILES])
        cnum = sb("cnum", [P, TOP * C])
        w8 = sb("w8", [P, E_])
        thr = sb("thr", [P, C])
        zero256 = sb("zero256", [P, C * E_])
        vt = sb("vt", [P, 6, TILES])
        idx = sb("idx", [P, TOP, TILES], I32)
        tef = sb("tef", [P, TILES])
        tile_e = sb("tile_e", [P, TILES], I32)
        gix = sb("gix", [P, RING, 1], I32)
        six = sb("six", [P, RING, 1], I32)
        XTf = XT[:].rearrange("p c i -> p (c i)")
        xg = XTf[:, 0:512].rearrange("p (n h) -> p n h", n=RING)
        xgT = XTf[:, 512:768].rearrange("p (n h) -> p n h", n=2)
        hs = XTf[:, 1024:2048].rearrange("p (n f) -> p n f", n=2)
        hg = XTf[:, 2048:3072].rearrange("p (n f) -> p n f", n=2)
        hT = XTf[:, 3072:4096].rearrange("p (n f) -> p n f", n=2)
        ys = sb("ys", [P, RING, P])
        Y1, Y2 = p2T, p3T
        xrows = nc.dram_tensor("xrows", (C * P, P), F32)
        yrows = nc.dram_tensor("yrows", ((TOP * C + TILES) * P, P), F32)
        g_in = [sem(f"g_in{i}") for i in range(RING)]
        sct = [sem(f"sct{i}") for i in range(RING)]

        s = {n: sem(n) for n in (
            "w_in xr_out tbn tst trs xln txl txlc lgt rt_ rex wk rank vmm ve idx_set te_set cst "
            "ftx fxc fm1 fad fge fth fhc fm2 fy fsi fgi pool_go y_in fin").split()}
        s |= {n: sem(n) for n in (
            "wts_in ones_set r_zero diag_in lnp_in braw_in x_in z2_in z3_in "
            "consts lnb_set bias_mm bsum_set b_step bb_set rs_set mh_set "
            "cen2 sq2 var2 sd2 rn2 zn2 cen3 sq3 var3 sd3 rn3 zn3 "
            "pr2 sg2 gate2 pr3 sg3 gate3 "
            "xbn xst xrs z1 amu acen asq avar ars anorm "
            "t1 t1c pra sga gata g5mm g5s tz tzc ein einc "
            "mu5 cen5 sq5 var5 rs5 norm5 t5 t5c pr5 u5 um5 ue5 y5 x2 out_done").split()}

        block = ctx.enter_context(nc.Block())
        x_v = x.rearrange("a c i j -> i (a c) j")
        out_v = out.rearrange("a c i j -> i (a c) j")

        def elu_exp(act, n):
            act.wait_ge(s["um5"], n + 1)
            if n >= 2:
                act.wait_ge(s["y5"], n - 1)
            act.activation(ue[:, n % 2, :], um[:, n % 2, :], ACT.Exp).then_inc(s["ue5"], 1)

        def elu_add(dve, n):
            U = sig5[:, 16 * n:16 * n + 16, :].rearrange("p j c -> p (j c)")
            dve.wait_ge(s["ue5"], n + 1)
            dve.scalar_tensor_tensor(U, ue[:, n % 2, :], -1.0, U, ALU.add, ALU.max).then_inc(s["y5"], 1)
            dve.wait_ge(s["y5"], n + 1)
            xs = X[:, :, 16 * n:16 * n + 16].rearrange("p c j -> p j c")
            dve.tensor_tensor(xs, xs, sig5[:, 16 * n:16 * n + 16, :], ALU.add).then_inc(s["x2"], 1)

        def row_stats(dve, eps, tag, base):
            me, mo, ve, vo = bn[:, :, 1], bn[:, :, 4], bn[:, :, 2], bn[:, :, 5]
            dve.tensor_tensor(st[:, 0, :], me, mo, ALU.add).then_inc(s[tag], 1)
            dve.tensor_tensor(st[:, 1, :], me, mo, ALU.subtract).then_inc(s[tag], 1)
            dve.tensor_tensor(st[:, 3, :], ve, vo, ALU.add).then_inc(s[tag], 1)
            dve.wait_ge(s[tag], base + 3)
            dve.tensor_scalar(st[:, 2, :], st[:, 0, :], 0.5, None, ALU.mult)
            dve.scalar_tensor_tensor(st[:, 4, :], st[:, 1, :], 0.25, st[:, 1, :], ALU.mult, ALU.mult)\
                .then_inc(s[tag], 1)
            dve.tensor_scalar(st[:, 7, :], st[:, 3, :], 1.0 / P, eps, ALU.mult, ALU.add).then_inc(s[tag], 1)
            dve.wait_ge(s[tag], base + 5)
            dve.tensor_tensor(st[:, 5, :], st[:, 7, :], st[:, 4, :], ALU.add).then_inc(s[tag], 1)

        def past(eng, signal, r, n):
            if not isinstance(r, int) or RING * r + n > 0:
                eng.wait_ge(signal, RING * r + n)

        def tiles(eng, *stages):
            def step(r, n):
                for stage, ahead in stages:
                    if not isinstance(r, int) or 0 <= RING * r + n + ahead < TILES:
                        stage(r, n + ahead)
            for n in range(-RING, RING):
                step(0, n)
            with eng.Fori(1, TILES // RING - 1) as r:
                for n in range(RING):
                    step(r, n)
            for n in range(RING):
                step(TILES // RING - 1, n)

        def logits(pe, n):
            pe.wait_ge(s["txlc"], n + 1)
            for c in range(4 * n, 4 * n + 4):
                mm = pe.matmul(bank[6][:, c * E_:(c + 1) * E_], XT[:, c, :], wg[:], start=True, stop=True)
            mm.then_inc(s["lgt"], 1)

        @block.sync
        def _(sp):
            sp.wait_ge(s["r_zero"], 1)
            for q in range(Q):
                sp.dma_start(R[q * C:(q + 1) * C, :, q, :], conv_w).then_inc(s["diag_in"], 16)
            for q in range(Q):
                sp.dma_start(lnp[q * C:(q + 1) * C, :, :], ln_p).then_inc(s["lnp_in"], 16)
            sp.dma_start(braw[:, :, :], conv_b.partition_broadcast(96)).then_inc(s["braw_in"], 16)
            for q in range(Q):
                sp.dma_start(Z2[q * C:(q + 1) * C, :, :], z2[0, :, q * C:(q + 1) * C, :]).then_inc(s["z2_in"], 16)
            sp.dma_start(X[:, :, :], x_v).then_inc(s["x_in"], 16)
            for q in range(Q):
                sp.dma_start(Z3[q * C:(q + 1) * C, :, :], z3[0, :, q * C:(q + 1) * C, :]).then_inc(s["z3_in"], 16)
            sp.dma_start(wg[:], W_g).then_inc(s["w_in"], 16)
            sp.dma_start(b2s[:], b2.rearrange("e h -> (e h)").partition_broadcast(P)).then_inc(s["w_in"], 16)
            sp.wait_ge(s["ein"], 8)
            sp.dma_start(w1s.rearrange("p (e f) -> p e f", e=E_), w1.rearrange("e h f -> h e f")).then_inc(s["w_in"], 16)
            sp.dma_start(w2s.rearrange("p (e k h) -> p e k h", e=E_, h=P), w2.rearrange("e (k p) h -> p e k h", p=P))\
                .then_inc(s["w_in"], 16)
            sp.dma_start(b1s, b1.rearrange("e f -> (e f)").partition_broadcast(P)).then_inc(s["w_in"], 16)
            xr = xrows.ap().rearrange("(c i) j -> i c j", i=P)
            for n in range(4):
                sp.wait_ge(s["xln"], 8 * n + 8)
                sp.dma_start(xr[:, 8 * n:8 * n + 8, :], XL[:, 8 * n:8 * n + 8, :]).then_inc(s["xr_out"], 16)
            for u in range(RING):
                sp.wait_ge(sct[u], 16 * (TILES // RING))
            yr = yrows.ap()[0:TOP * C * P, :].rearrange("(k c i) j -> k i c j", k=TOP, i=P)
            for n in range(4):
                for k, Y in enumerate((Y1, Y2)):
                    sp.dma_start(Y[:, 8 * n:8 * n + 8, :], yr[k][:, 8 * n:8 * n + 8, :]).then_inc(s["y_in"], 16)
            for n in range(4):
                sp.wait_ge(s["fin"], 16 * (n + 1))
                sp.dma_start(out_v[:, 8 * n:8 * n + 8, :], X[:, 8 * n:8 * n + 8, :]).then_inc(s["out_done"], 16)
            sp.wait_ge(s["out_done"], 64)

        @block.gpsimd
        def _(pool):
            pool.memset(R[:], 0.0).then_inc(s["r_zero"], 1)
            pool.memset(ident[:], 0.0).then_inc(s["ones_set"], 1)
            pool.wait_ge(s["ones_set"], 1)
            pool.affine_select(out=ident[:], in_=ident[:], compare_op=ALU.not_equal, fill=1.0, base=0,
                               pattern=[[-1, P]], channel_multiplier=1).then_inc(s["ones_set"], 1)
            pool.memset(lower[:], 1.0).then_inc(s["cst"], 1)
            pool.wait_ge(s["cst"], 1)
            pool.affine_select(out=lower[:], in_=lower[:], compare_op=ALU.is_gt, fill=0.0, base=0,
                               pattern=[[1, P]], channel_multiplier=-1).then_inc(s["cst"], 1)
            imp = dict(allow_small_or_imprecise_dtypes=True)
            pool.iota(iota_w[:], pattern=[[1, P]], base=0, channel_multiplier=0, **imp).then_inc(s["cst"], 1)
            pool.iota(iota_p[:], pattern=[[0, 1]], base=0, channel_multiplier=1, **imp).then_inc(s["cst"], 1)
            pool.iota(spare[:], pattern=[[P, TILES]], base=(TOP * C + 1) * P, channel_multiplier=1, **imp)\
                .then_inc(s["cst"], 1)
            pool.iota(cnum[:], pattern=[[1, TOP * C]], base=1, channel_multiplier=0, **imp).then_inc(s["cst"], 1)
            pool.iota(w8[:], pattern=[[-1, E_]], base=E_, channel_multiplier=0, **imp).then_inc(s["cst"], 1)
            pool.iota(thr[:], pattern=[[P, C]], base=0, channel_multiplier=0, **imp).then_inc(s["cst"], 1)
            pool.wait_ge(s["mh_set"], 4)
            pool.wait_ge(s["xst"], 6)
            pool.tensor_tensor(st[:, 6, :], st[:, 5, :], mhalf[:], ALU.pow).then_inc(s["xrs"], 1)
            for k in range(NCH):
                pool.wait_ge(s["avar"], 2 * k + 2)
                d = slice(k * CH, (k + 1) * CH)
                pool.tensor_tensor(rsd[:, d], var[:, d], mhalf[:], ALU.pow).then_inc(s["ars"], 1)
            for k in range(NCH):
                pool.wait_ge(s["var5"], 2 * k + 2)
                d = slice(k * CH, (k + 1) * CH)
                pool.tensor_tensor(rsd[:, d], var[:, d], mhalf[:], ALU.pow).then_inc(s["rs5"], 1)
            pool.wait_ge(s["tst"], 6)
            pool.tensor_tensor(st[:, 6, :], st[:, 5, :], mhalf[:], ALU.pow).then_inc(s["trs"], 1)

            def gather(r, n):
                pool.wait_ge(s["fgi"], RING * r + n + 1)
                past(pool, s["ftx"], r, n - RING + 1)
                pool.sem_inc(s["pool_go"], 1)
                pool.indirect_dma_start(out=xg[:, n % RING, :], out_offset=None, in_=xrows.ap(),
                                        in_offset=bass.IndirectOffsetOnAxis(ap=gix[:, n % RING, :], axis=0))\
                    .then_inc(g_in[n % RING], 16)

            def scatter(r, n):
                pool.wait_ge(s["fsi"], 4 * r + n + 1)
                pool.wait_ge(s["fy"], 4 * r + n + 1)
                pool.sem_inc(s["pool_go"], 1)
                pool.indirect_dma_start(out=yrows.ap(), in_=ys[:, n % RING, :], in_offset=None,
                                        out_offset=bass.IndirectOffsetOnAxis(ap=six[:, n % RING, :], axis=0))\
                    .then_inc(sct[n % RING], 16)

            pool.wait_ge(s["xr_out"], 64)
            tiles(pool, (scatter, 0), (gather, RING))

        @block.tensor
        def _(pe):
            pe.wait_ge(s["diag_in"], 64)
            pe.wait_ge(s["lnb_set"], 4)
            for n, (g, a, b, bk) in enumerate([(0, 0, 4, 0), (0, 4, 5, 1), (1, 5, 7, 2), (2, 7, 9, 3), (3, 9, 10, 4)]):
                pe.matmul(bank[bk][0:96, 0:(b - a) * P], lnb[:, g, :], R[:, a:b].rearrange("p s q c -> p (s q c)"),
                          start=True, stop=True).then_inc(s["bias_mm"], 1)

            def norm(zin, z, tag):
                pe.wait_ge(s["consts"], 1)
                pe.wait_ge(s[zin], 64)

                def centre(n):
                    if n >= 2:
                        pe.wait_ge(s["zn" + tag], n - 1)
                    pe.matmul(bank[n % 2][:, :], cen[:], z[:, 4 * n:4 * n + 4, :].rearrange("p i j -> p (i j)"),
                              start=True, stop=True).then_inc(s["cen" + tag], 1)
                centre(0)
                for n in range(8):
                    if n < 7:
                        centre(n + 1)
                    pe.wait_ge(s["sq" + tag], n + 1)
                    if n >= 2:
                        pe.wait_ge(s["sd" + tag], n - 1)
                    pe.matmul(bank[2 + n % 2][:, :], blk[:], sq[:, n % 2, :], start=True, stop=True)\
                        .then_inc(s["var" + tag], 1)

            def proj(z, tag, a, m, before):
                if before + m >= 4:
                    pe.wait_ge(s["gate2"], min(16, before + m - 3))
                    if before + m - 3 > 16:
                        pe.wait_ge(s["gate3"], before + m - 3 - 16)
                pe.wait_ge(s["zn" + tag], m // 2 + 1)
                pe.wait_ge(s["bb_set"], 3)
                pe.wait_ge(s["rs_set"], 4)
                for h in range(2):
                    o = bank[4 + m % 4][:, 256 * h:256 * h + 256]
                    pe.matmul(o, z[:, 2 * m + h, :], RS[:, a:a + 2].rearrange("p s q c -> p (s q c)"),
                              start=True, stop=False)
                    mm = pe.matmul(o, pick3[:], BB[:, a * P:(a + 2) * P], start=False, stop=True)
                mm.then_inc(s["pr" + tag], 1)

            pe.wait_ge(s["bsum_set"], 5)
            norm("z2_in", Z2, "2")
            for m in range(16):
                proj(Z2, "2", 5, m, 0)
            norm("z3_in", Z3, "3")

            def t1(k):
                pe.wait_ge(s["anorm"], k + 1)
                for h in range(2):
                    n = 2 * k + h
                    if n >= 2:
                        pe.wait_ge(s["t1c"], n - 1)
                    else:
                        pe.wait_ge(s["zn3"], 8)
                    for v in range(4):
                        j0 = (4 * n + v) * 4
                        mm = pe.transpose(bank[n % 2][:, v * P:(v + 1) * P],
                                          ZD[:, j0:j0 + 4, :].rearrange("p j c -> p (j c)"), ident[:])
                    mm.then_inc(s["t1"], 1)
            for m in range(16):
                proj(Z3, "3", 7, m, 16)
                if m % 4 == 0 and m:
                    t1(m // 4 - 1)
            t1(3)
            for n in range(C):
                pe.wait_ge(s["t1c"], n // 4 + 1)
                if n >= 4:
                    pe.wait_ge(s["gata"], n - 3)
                else:
                    pe.wait_ge(s["gate3"], 13 + n)
                pe.matmul(bank[4 + n % 4][:, :], ZB[:, n, :], RS[:, 0:4].rearrange("p s q c -> p (s q c)"),
                          start=True, stop=False)
                pe.matmul(bank[4 + n % 4][:, :], pick3[:], BB[:, 0:512], start=False, stop=True)\
                    .then_inc(s["pra"], 1)
                g = n // 4
                if n % 4 == 0:
                    if g >= 2:
                        pe.wait_ge(s["g5s"], g - 1)
                    else:
                        pe.wait_ge(s["zn3"], 8)
                o = bank[2 + g % 2][:, (n % 4) * P:(n % 4 + 1) * P]
                pe.matmul(o, ZB[:, n, :], RS[:, 4].rearrange("p q c -> p (q c)"), start=True, stop=False)
                mm = pe.matmul(o, pick3[:], BB[:, 512:640], start=False, stop=True)
                if n % 4 == 3:
                    mm.then_inc(s["g5mm"], 1)
            pe.wait_ge(s["gata"], C)
            for n in range(8):
                pe.wait_ge(s["tzc"] if n >= 2 else s["t1c"], n - 1 if n >= 2 else 8)
                for v in range(4):
                    mm = pe.transpose(bank[n % 2][:, v * P:(v + 1) * P], z13[:, 4 * n + v, :], ident[:])
                mm.then_inc(s["tz"], 1)
            for n in range(8):
                pe.wait_ge(s["tzc"], n + 1)
                if n >= 4:
                    pe.wait_ge(s["einc"], n - 3)
                for v in range(4):
                    c = 4 * n + v
                    o = bank[4 + n % 4][:, v * P:(v + 1) * P]
                    pe.matmul(o, p2T[:, c, :], z12[:, c, :], start=True, stop=False)
                    mm = pe.matmul(o, ZD[:].rearrange("p a b -> p (a b)")[:, c * P:(c + 1) * P], p3T[:, c, :],
                                   start=False, stop=True)
                mm.then_inc(s["ein"], 1)
            def t5(n):
                pe.wait_ge(s["norm5"], n // 2 + 1)
                if n >= 2:
                    pe.wait_ge(s["t5c"], n - 1)
                for v in range(4):
                    j0 = (4 * n + v) * 4
                    mm = pe.transpose(bank[n % 2][:, v * P:(v + 1) * P],
                                      p3j[:, j0:j0 + 4, :].rearrange("p j c -> p (j c)"), ident[:])
                mm.then_inc(s["t5"], 1)
            t5(0)
            for n in range(8):
                if n < 7:
                    t5(n + 1)
                pe.wait_ge(s["t5c"], n + 1)
                if n >= 2:
                    pe.wait_ge(s["u5"], n - 1)
                for v in range(4):
                    o = bank[2 + n % 2][:, v * P:(v + 1) * P]
                    pe.matmul(o, T5[:, 4 * n + v, :], RS[:, 9].rearrange("p q c -> p (q c)"), start=True, stop=False)
                    mm = pe.matmul(o, pick3[:], BB[:, 9 * P:10 * P], start=False, stop=True)
                mm.then_inc(s["pr5"], 1)
            for n in range(8):
                pe.wait_ge(s["xln"], 4 * n + 4)
                if n >= 2:
                    pe.wait_ge(s["txlc"], n - 1)
                for v in range(4):
                    mm = pe.transpose(bank[4 + n % 2][:, v * P:(v + 1) * P], XL[:, 4 * n + v, :], ident[:])
                mm.then_inc(s["txl"], 1)
                if n == 0:
                    pe.wait_ge(s["w_in"], 80)
                else:
                    logits(pe, n - 1)
            logits(pe, 7)
            pe.wait_ge(s["wk"], 1)
            pe.wait_ge(s["mh_set"], 14)
            pe.matmul(bank[7][:, 0:256], lower[:], M_[:], start=True, stop=True)
            pe.matmul(bank[7][:, 256:512], ones[:], M_[:], start=True, stop=True).then_inc(s["rank"], 1)
            pe.wait_ge(s["vmm"], 4)
            for n in range(TOP * C):
                mm = pe.matmul(bank[0][:, 0:2 * TILES], BH[:, n, :], AW[:, n].rearrange("p t a -> p (t a)"),
                               start=(n == 0), stop=(n == TOP * C - 1))
            mm.then_inc(s["ve"], 1)
            pe.wait_ge(s["te_set"], 5)

            def x_turn(r, n):
                pe.wait_ge(g_in[n % RING], 16 * (r + n // RING + 1))
                past(pe, s["fxc"], r, n - 1)
                pe.transpose(bank[n % 2][:, 0:P], xg[:, n % RING, :], ident[:]).then_inc(s["ftx"], 1)

            def expert(r, n):
                return pe.value_load(tile_e[0:1, bass.ds(RING * r + n, 1)], min_val=0, max_val=E_ - 1)

            def up(r, n):
                e = expert(r, n)
                pe.wait_ge(s["fxc"], RING * r + n + 1)
                past(pe, s["fad"], r, n - 1)
                pe.matmul(bank[2 + n % 2][:, :], xgT[:, n % 2, :], w1s[:, bass.ds(e * F, F)], start=True, stop=True)\
                    .then_inc(s["fm1"], 1)

            def h_turn(r, n):
                pe.wait_ge(s["fge"], RING * r + n + 1)
                past(pe, s["fhc"], r, n - 1)
                for k in range(4):
                    mm = pe.transpose(bank[4 + n % 2][:, k * P:(k + 1) * P], hg[:, n % 2, k * P:(k + 1) * P], ident[:])
                mm.then_inc(s["fth"], 1)

            def down(r, n):
                e = expert(r, n)
                pe.wait_ge(s["fhc"], RING * r + n + 1)
                past(pe, s["fy"], r, n - 1)
                for k in range(4):
                    mm = pe.matmul(bank[6 + n % 2][:, 0:P], hT[:, n % 2, k * P:(k + 1) * P],
                                   w2s[:, bass.ds(e * F + k * P, P)], start=(k == 0), stop=(k == 3))
                mm.then_inc(s["fm2"], 1)

            tiles(pe, (x_turn, 3), (up, 2), (h_turn, 1), (down, 0))

        @block.scalar
        def _(act):
            def norm(tag):
                act.wait_ge(s["mh_set"], 7)

                def square(n):
                    act.wait_ge(s["cen" + tag], n + 1)
                    if n >= 2:
                        act.wait_ge(s["var" + tag], n - 1)
                    act.activation(sq[:, n % 2, :], bank[n % 2][:, :], ACT.Square).then_inc(s["sq" + tag], 1)
                square(0)
                for n in range(8):
                    if n < 7:
                        square(n + 1)
                    act.wait_ge(s["var" + tag], n + 1)
                    if n >= 2:
                        act.wait_ge(s["rn" + tag], n - 1)
                    act.activation(sd[:, n % 2, :], bank[2 + n % 2][:, :], ACT.Sqrt, bias=epsc[:, 0:1])\
                        .then_inc(s["sd" + tag], 1)

            def sigma(tag, m, before):
                act.wait_ge(s["pr" + tag], m + 1)
                if m >= 2:
                    act.wait_ge(s["gate" + tag], m - 1)
                elif before:
                    act.wait_ge(s["gate2"], 15 + m)
                act.activation(sg[:, m % 2, :].rearrange("p (h n) -> p h n", h=2),
                               bank[4 + m % 4][:].rearrange("p (h t n) -> p h t n", h=2, t=2)[:, :, 1, :],
                               ACT.Sigmoid).then_inc(s["sg" + tag], 1)

            norm("2")
            for m in range(16):
                sigma("2", m, 0)
            norm("3")

            def t1_copy(n):
                act.wait_ge(s["t1"], n + 1)
                act.activation(ZB[:, 4 * n:4 * n + 4, :].rearrange("p a b -> p (a b)"), bank[n % 2][:, :], ACT.Copy)\
                    .then_inc(s["t1c"], 1)
            for m in range(16):
                sigma("3", m, 16)
                if m % 4 == 1:
                    k = m // 4
                    act.wait_ge(s["acen"], k + 1)
                    if k:
                        act.wait_ge(s["avar"], 2 * k - 1)
                    act.activation(Asq[:, :], ZA[:, :, k * CH:(k + 1) * CH].rearrange("p c j -> p j c"),
                                   ACT.Square).then_inc(s["asq"], 1)
                if m % 4 == 0 and m:
                    for h in range(2):
                        t1_copy(2 * (m // 4 - 1) + h)
            for h in range(2):
                t1_copy(6 + h)
            for n in range(C):
                act.wait_ge(s["pra"], n + 1)
                if n >= 2:
                    act.wait_ge(s["gata"], n - 1)
                else:
                    act.wait_ge(s["gate3"], 15 + n)
                act.activation(sg[:, n % 2, :].rearrange("p (h n) -> p h n", h=2),
                               bank[4 + n % 4][:].rearrange("p (h t n) -> p h t n", h=2, t=2)[:, :, 1, :],
                               ACT.Sigmoid).then_inc(s["sga"], 1)
                if n % 4 == 3:
                    g = n // 4
                    act.wait_ge(s["g5mm"], g + 1)
                    act.activation(sig5[:, 16 * g:16 * g + 16, :].rearrange("p j c -> p (j c)"),
                                   bank[2 + g % 2][:, :], ACT.Sigmoid).then_inc(s["g5s"], 1)
            for n in range(8):
                act.wait_ge(s["tz"], n + 1)
                act.activation(ZD[:].rearrange("p a b -> p (a b)")[:, 512 * n:512 * n + 512], bank[n % 2][:, :],
                               ACT.Copy).then_inc(s["tzc"], 1)
            for n in range(8):
                act.wait_ge(s["ein"], n + 1)
                act.activation(Zt[:, 4 * n:4 * n + 4, :].rearrange("p a b -> p (a b)"), bank[4 + n % 4][:, :],
                               ACT.Copy).then_inc(s["einc"], 1)
            for k in range(NCH):
                act.wait_ge(s["cen5"], k + 1)
                if k:
                    act.wait_ge(s["var5"], 2 * k - 1)
                act.activation(Asq[:, :], Zt[:, :, k * CH:(k + 1) * CH].rearrange("p c j -> p j c"), ACT.Square)\
                    .then_inc(s["sq5"], 1)
            for n in range(8):
                act.wait_ge(s["t5"], n + 1)
                act.activation(T5[:, 4 * n:4 * n + 4, :].rearrange("p a b -> p (a b)"), bank[n % 2][:, :],
                               ACT.Copy).then_inc(s["t5c"], 1)
                if n:
                    elu_exp(act, n - 1)
            elu_exp(act, 7)
            for n in range(8):
                act.wait_ge(s["txl"], n + 1)
                act.activation(XT[:, 4 * n:4 * n + 4, :].rearrange("p a b -> p (a b)"), bank[4 + n % 2][:, :],
                               ACT.Copy).then_inc(s["txlc"], 1)
            act.wait_ge(s["rt_"], 2)
            act.activation(rt[:, 1, :], rt[:, 0, :], ACT.Exp).then_inc(s["rex"], 1)
            act.wait_ge(s["te_set"], 5)

            def gelu(r, n):
                act.wait_ge(s["fad"], RING * r + n + 1)
                past(act, s["fth"], r, n - 1)
                act.activation(hg[:, n % 2, :], hs[:, n % 2, :], ACT.Gelu).then_inc(s["fge"], 1)

            def h_copy(r, n):
                act.wait_ge(s["fth"], RING * r + n + 1)
                past(act, s["fm2"], r, n - 1)
                act.activation(hT[:, n % 2, :], bank[4 + n % 2][:, :], ACT.Copy).then_inc(s["fhc"], 1)

            tiles(act, (gelu, 2), (h_copy, 1))

        @block.vector
        def _(dve):
            dve.memset(mhalf[:], -0.5).then_inc(s["mh_set"], 1)
            dve.memset(pick3[:], 0.0).then_inc(s["mh_set"], 1)
            dve.memset(epsc[:], EPS).then_inc(s["mh_set"], 1)
            dve.memset(BB[:], 0.0).then_inc(s["mh_set"], 1)
            dve.memset(ones[:], 1.0).then_inc(s["mh_set"], 1)
            dve.memset(zero256[:], 0.0).then_inc(s["mh_set"], 1)
            dve.memset(blk[:], 0.0).then_inc(s["mh_set"], 1)
            dve.wait_ge(s["mh_set"], 7)
            for k in range(3):
                dve.memset(pick3[32 * k:32 * k + 1, :], 1.0).then_inc(s["mh_set"], 1)
            for q in range(Q):
                d = slice(q * C, (q + 1) * C)
                dve.memset(blk[d, d], 1.0 / C).then_inc(s["mh_set"], 1)
            dve.wait_ge(s["ones_set"], 2)
            dve.wait_ge(s["mh_set"], 10 + Q)
            dve.tensor_tensor(cen[:], ident[:], blk[:], ALU.subtract).then_inc(s["consts"], 1)
            dve.wait_ge(s["lnp_in"], 64)
            for g in range(4):
                dve.tensor_copy(lnb[:, g, :], lnp[:, g, 1:2].to_broadcast([P, 96])).then_inc(s["lnb_set"], 1)
            dve.wait_ge(s["diag_in"], 64)
            for g, (a, b) in enumerate(GROUPS):
                dve.tensor_scalar(RS[:, a:b], R[:, a:b], lnp[:, g, 0:1], None, ALU.mult).then_inc(s["rs_set"], 1)
            dve.wait_ge(s["braw_in"], 16)
            for n, (a, b, bk) in enumerate([(0, 4, 0), (4, 5, 1), (5, 7, 2), (7, 9, 3), (9, 10, 4)]):
                dve.wait_ge(s["bias_mm"], n + 1)
                dve.tensor_tensor(bsum[:, a:b], bank[bk][0:96, 0:(b - a) * P].rearrange("p (s q c) -> p s q c", q=Q, c=C),
                                  braw[:, a:b].unsqueeze(2).to_broadcast([96, b - a, Q, C]), ALU.add)\
                    .then_inc(s["bsum_set"], 1)
            dve.wait_ge(s["bsum_set"], 5)
            bs = bsum[:].rearrange("p s q c -> p (s q c)")
            dve.tensor_copy(bhi[:], bs).then_inc(s["b_step"], 1)
            dve.wait_ge(s["b_step"], 1)
            dve.tensor_tensor(bs, bs, bhi[:], ALU.subtract).then_inc(s["b_step"], 1)
            dve.wait_ge(s["b_step"], 2)
            dve.tensor_copy(bmid[:], bs).then_inc(s["b_step"], 1)
            dve.wait_ge(s["b_step"], 3)
            dve.tensor_tensor(bs, bs, bmid[:], ALU.subtract).then_inc(s["b_step"], 1)
            dve.wait_ge(s["mh_set"], 7)
            dve.wait_ge(s["b_step"], 4)
            dve.tensor_copy(BB[0:1, :], bhi[0:1, :]).then_inc(s["bb_set"], 1)
            dve.tensor_copy(BB[32:33, :], bmid[32:33, :]).then_inc(s["bb_set"], 1)
            dve.tensor_copy(BB[64:65, :], bs[64:65, :]).then_inc(s["bb_set"], 1)

            def norm(z, tag, n):
                dve.wait_ge(s["sd" + tag], n + 1)
                dve.reciprocal(rn[:, n % 2, :], sd[:, n % 2, :]).then_inc(s["rn" + tag], 1)
                dve.wait_ge(s["rn" + tag], n + 1)
                dve.tensor_tensor(z[:, 4 * n:4 * n + 4, :].rearrange("p i j -> p (i j)"), bank[n % 2][:, :],
                                  rn[:, n % 2, :], ALU.mult).then_inc(s["zn" + tag], 1)

            def gate(dst, tag, m):
                dve.wait_ge(s["sg" + tag], m + 1)
                for h in range(2):
                    ins = dve.tensor_tensor(
                        dst[:].rearrange("p c (q i) -> p i q c", q=Q)[:, 2 * m + h],
                        bank[4 + m % 4][:, 256 * h:256 * h + P].rearrange("p (q c) -> p q c", q=Q),
                        sg[:, m % 2, h * P:(h + 1) * P].rearrange("p (q c) -> p q c", q=Q), ALU.mult)
                ins.then_inc(s["gate" + tag], 1)

            for n in range(8):
                norm(Z2, "2", n)
            dve.wait_ge(s["x_in"], 16)
            for m in range(16):
                gate(p2T, "2", m)
                for c in (2 * m, 2 * m + 1):
                    dve.bn_stats(bn[:, c, :], X[:, c, :]).then_inc(s["xbn"], 1)
            dve.wait_ge(s["xbn"], C)
            row_stats(dve, EPS_C, "xst", 0)
            for n in range(8):
                norm(Z3, "3", n)
                if n == 0:
                    dve.wait_ge(s["xrs"], 1)
                for c in range(4 * n, 4 * n + 4):
                    dve.tensor_scalar(ZA[:, c, :], X[:, c, :], st[:, 2, c:c + 1], st[:, 6, c:c + 1],
                                      ALU.subtract, ALU.mult).then_inc(s["z1"], 1)

            def channel_mean(src, k, tag):
                d = slice(k * CH, (k + 1) * CH)
                dve.tensor_reduce(mu[:, d], src[:, :, d].rearrange("p c j -> p j c"), AX.X, ALU.add)\
                    .then_inc(s[tag], 1)
                dve.wait_ge(s[tag], 2 * k + 1)
                dve.tensor_scalar(mu[:, d], mu[:, d], 1.0 / C, None, ALU.mult).then_inc(s[tag], 1)

            def channel_centre(src, k, tag_mu, tag):
                d = slice(k * CH, (k + 1) * CH)
                dve.wait_ge(s[tag_mu], 2 * k + 2)
                dve.tensor_tensor(src[:, :, d], src[:, :, d], mu[:, d].unsqueeze(1).to_broadcast([P, C, CH]),
                                  ALU.subtract).then_inc(s[tag], 1)

            def channel_var(k, tag_sq, tag):
                d = slice(k * CH, (k + 1) * CH)
                dve.wait_ge(s[tag_sq], k + 1)
                dve.tensor_reduce(var[:, d], Asq[:].rearrange("p (j c) -> p j c", c=C), AX.X, ALU.add)\
                    .then_inc(s[tag], 1)
                dve.wait_ge(s[tag], 2 * k + 1)
                dve.tensor_scalar(var[:, d], var[:, d], 1.0 / C, EPS, ALU.mult, ALU.add).then_inc(s[tag], 1)

            def channel_norm(dst, src, k, tag_rs, tag):
                d = slice(k * CH, (k + 1) * CH)
                dve.wait_ge(s[tag_rs], k + 1)
                dve.tensor_tensor(dst[:, d, :], src[:, :, d].rearrange("p c j -> p j c"),
                                  rsd[:, d].unsqueeze(2).to_broadcast([P, CH, C]), ALU.mult).then_inc(s[tag], 1)

            dve.wait_ge(s["z1"], C)
            for m in range(16):
                gate(p3T, "3", m)
                k = m // 4
                if m % 4 == 0:
                    channel_mean(ZA, k, "amu")
                if m % 4 == 1:
                    channel_centre(ZA, k, "amu", "acen")
                if m % 4 == 2:
                    channel_var(k, "asq", "avar")
                if m % 4 == 3:
                    channel_norm(ZD, ZA, k, "ars", "anorm")
            for n in range(C):
                dve.wait_ge(s["sga"], n + 1)
                for h in range(2):
                    ins = dve.tensor_tensor(
                        Z23[:, h, :, 4 * n:4 * n + 4].rearrange("p c j -> p j c"),
                        bank[4 + n % 4][:, 256 * h:256 * h + P].rearrange("p (j c) -> p j c", c=C),
                        sg[:, n % 2, h * P:(h + 1) * P].rearrange("p (j c) -> p j c", c=C), ALU.mult)
                ins.then_inc(s["gata"], 1)
            dve.wait_ge(s["einc"], 8)
            for k in range(NCH):
                channel_mean(Zt, k, "mu5")
                channel_centre(Zt, k, "mu5", "cen5")
                channel_var(k, "sq5", "var5")
                channel_norm(p3j, Zt, k, "rs5", "norm5")
            for n in range(8):
                dve.wait_ge(s["pr5"], n + 1)
                if n >= 2:
                    dve.wait_ge(s["ue5"], n - 1)
                dve.wait_ge(s["g5s"], 8)
                U = sig5[:, 16 * n:16 * n + 16, :].rearrange("p j c -> p (j c)")
                dve.tensor_tensor(U, bank[2 + n % 2][:, :], U, ALU.mult).then_inc(s["u5"], 1)
                dve.wait_ge(s["u5"], n + 1)
                dve.tensor_scalar(um[:, n % 2, :], U, 0.0, None, ALU.min).then_inc(s["um5"], 1)
                if n:
                    elu_add(dve, n - 1)
            elu_add(dve, 7)
            dve.wait_ge(s["x2"], 8)
            for c in range(C):
                dve.bn_stats(bn[:, c, :], X[:, c, :]).then_inc(s["tbn"], 1)
            dve.wait_ge(s["tbn"], C)
            row_stats(dve, EPS, "tst", 0)
            dve.wait_ge(s["trs"], 1)
            for c in range(C):
                dve.tensor_scalar(XL[:, c, :], X[:, c, :], st[:, 2, c:c + 1], st[:, 6, c:c + 1],
                                  ALU.subtract, ALU.mult).then_inc(s["xln"], 1)
            done = [0]

            def step(ins):
                ins.then_inc(s["rt_"], 1)
                done[0] += 1
                dve.wait_ge(s["rt_"], done[0])

            def ce(k):
                return rt[:, k, :].rearrange("p (c e) -> p c e", e=E_)

            def over_e(v):
                return v.unsqueeze(2).to_broadcast([P, C, E_])

            def over_c(v):
                return v.unsqueeze(1).to_broadcast([P, C, E_])

            dve.wait_ge(s["cst"], 8)
            dve.wait_ge(s["lgt"], 8)
            L = bank[6][:, 0:256].rearrange("p (c e) -> p c e", e=E_)
            step(dve.tensor_reduce(rs_[:, 0, :], L, AX.X, ALU.max))
            step(dve.tensor_tensor(ce(0), L, over_e(rs_[:, 0, :]), ALU.subtract))
            dve.wait_ge(s["rex"], 1)
            step(dve.tensor_reduce(rs_[:, 1, :], ce(1), AX.X, ALU.add))
            step(dve.reciprocal(rs_[:, 2, :], rs_[:, 1, :]))
            step(dve.tensor_tensor(ce(2), ce(1), over_e(rs_[:, 2, :]), ALU.mult))
            for k in range(TOP):
                src, hot = ce(2 + k), ce(4 + k)
                step(dve.tensor_reduce(prob[:, k, :], src, AX.X, ALU.max))
                step(dve.tensor_tensor(ce(6), src, over_e(prob[:, k, :]), ALU.is_equal))
                step(dve.tensor_tensor(ce(6), ce(6), over_c(w8[:]), ALU.mult))
                step(dve.tensor_reduce(rs_[:, 3, :], ce(6), AX.X, ALU.max))
                step(dve.tensor_tensor(hot, over_c(w8[:]), over_e(rs_[:, 3, :]), ALU.is_equal))
                if k + 1 < TOP:
                    step(dve.scalar_tensor_tensor(ce(3), hot, -2.0, src, ALU.mult, ALU.add))
            dve.tensor_tensor(M_[:], rt[:, 4, :], rt[:, 5, :], ALU.add).then_inc(s["wk"], 1)
            dve.wait_ge(s["rank"], 1)
            ec = [rt[:, k, :].rearrange("p (e c) -> p e c", c=C) for k in range(12)]
            step(dve.tensor_copy(ec[6], bank[7][:, 256:512].rearrange("p (c e) -> p e c", e=E_)))
            step(dve.tensor_tensor_scan(rt[:, 7, :], rt[:, 6, :], zero256[:], 0.0, ALU.add, ALU.add))
            step(dve.tensor_tensor(rt[:, 8, :], rt[:, 7, :], rt[:, 6, :], ALU.subtract))
            step(dve.tensor_tensor(re_[:, 0, :], ec[7][:, :, C - 1], ec[8][:, :, 0], ALU.subtract))
            step(dve.tensor_tensor(ec[9], re_[:, 0, :].unsqueeze(2).to_broadcast([P, E_, C]),
                                   thr[:].unsqueeze(1).to_broadcast([P, E_, C]), ALU.is_gt))
            step(dve.tensor_reduce(re_[:, 1, :], ec[9], AX.X, ALU.add))
            step(dve.tensor_tensor_scan(re_[:, 2, :], re_[:, 1, :], zero256[:, 0:E_], 0.0, ALU.add, ALU.add))
            step(dve.tensor_tensor(re_[:, 3, :], re_[:, 2, :], re_[:, 1, :], ALU.subtract))
            step(dve.scalar_tensor_tensor(re_[:, 4, :], re_[:, 3, :], float(P), ec[8][:, :, 0], ALU.mult, ALU.subtract))
            step(dve.tensor_tensor(ec[10], ec[8], re_[:, 4, :].unsqueeze(2).to_broadcast([P, E_, C]), ALU.add))
            step(dve.tensor_tensor(ce(11), bank[7][:, 0:256].rearrange("p (c e) -> p c e", e=E_),
                                   rt[:, 10, :].rearrange("p (e c) -> p c e", c=C), ALU.add))
            for k in range(TOP):
                step(dve.tensor_tensor(ce(6), ce(4 + k), ce(11), ALU.mult))
                step(dve.tensor_reduce(slot[:, k, :], ce(6), AX.X, ALU.add))
            step(dve.tensor_copy(sloti[:, 0, :], slot[:].rearrange("p k c -> p (k c)")))
            step(dve.tensor_scalar(sloti[:, 1, :], sloti[:, 0, :], 7, None, ALU.logical_shift_right))
            step(dve.tensor_scalar(sloti[:, 2, :], sloti[:, 0, :], P - 1, None, ALU.bitwise_and))
            step(dve.tensor_copy(slota[:], sloti[:, 1:3, :]))
            n2 = TOP * C
            dve.tensor_tensor(BH, slota[:, 1, :].unsqueeze(2).to_broadcast([P, n2, P]),
                              iota_w[:].unsqueeze(1).to_broadcast([P, n2, P]), ALU.is_equal).then_inc(s["vmm"], 1)
            dve.tensor_tensor(AW[:, :, 0, :], slota[:, 0, :].unsqueeze(2).to_broadcast([P, n2, TILES]),
                              iota_w[:, 0:TILES].unsqueeze(1).to_broadcast([P, n2, TILES]), ALU.is_equal)\
                .then_inc(s["vmm"], 1)
            dve.wait_ge(s["vmm"], 2)
            dve.tensor_scalar(AW[:, :, 1, :], AW[:, :, 0, :], iota_p[:, 0:1], None, ALU.mult).then_inc(s["vmm"], 1)
            dve.wait_ge(s["vmm"], 3)
            dve.tensor_tensor(AW[:, :, 0, :], AW[:, :, 0, :], cnum[:].unsqueeze(2).to_broadcast([P, n2, TILES]),
                              ALU.mult).then_inc(s["vmm"], 1)
            dve.tensor_tensor(te, re_[:, 2, :].unsqueeze(1).to_broadcast([P, TILES, E_]),
                              iota_w[:, 0:TILES].unsqueeze(2).to_broadcast([P, TILES, E_]), ALU.is_le)\
                .then_inc(s["te_set"], 1)
            dve.wait_ge(s["te_set"], 1)
            dve.tensor_reduce(tef[:], te, AX.X, ALU.add).then_inc(s["te_set"], 1)
            dve.wait_ge(s["te_set"], 2)
            dve.tensor_scalar(tile_e[:], tef[:], float(E_ - 1), None, ALU.min).then_inc(s["te_set"], 1)
            dve.wait_ge(s["ve"], 1)
            step(dve.tensor_copy(vt[:, 0, :], bank[0][:, TILES:2 * TILES]))
            step(dve.scalar_tensor_tensor(vt[:, 1, :], bank[0][:, 0:TILES], float(P), vt[:, 0, :], ALU.mult, ALU.add))
            step(dve.scalar_tensor_tensor(vt[:, 2, :], vt[:, 1, :], float(P), spare[:], ALU.is_lt, ALU.mult))
            step(dve.tensor_scalar(vt[:, 3, :], vt[:, 1, :], -float(P), None, ALU.add))
            dve.tensor_tensor(idx[:, 1, :], vt[:, 3, :], vt[:, 2, :], ALU.add).then_inc(s["te_set"], 1)
            step(dve.tensor_scalar(vt[:, 5, :], vt[:, 3, :], 0.0, None, ALU.max))
            step(dve.tensor_scalar(vt[:, 4, :], vt[:, 5, :], float(C * P), -float(C * P), ALU.is_ge, ALU.mult))
            dve.tensor_tensor(idx[:, 0, :], vt[:, 5, :], vt[:, 4, :], ALU.add).then_inc(s["te_set"], 1)
            dve.wait_ge(s["te_set"], 5)
            dve.wait_ge(s["w_in"], 80)

            def gather_index(r, n):
                if not isinstance(r, int) or RING * r + n >= RING:
                    dve.wait_ge(g_in[n % RING], 16 * (r + n // RING))
                dve.tensor_copy(gix[:, n % RING, :], idx[:, 0, bass.ds(RING * r + n, 1)]).then_inc(s["fgi"], 1)

            def scatter_index(r, n):
                if not isinstance(r, int) or RING * r + n >= RING:
                    dve.wait_ge(sct[n % RING], 16 * (r + n // RING))
                dve.tensor_copy(six[:, n % RING, :], idx[:, 1, bass.ds(RING * r + n, 1)]).then_inc(s["fsi"], 1)

            def x_copy(r, n):
                dve.wait_ge(s["ftx"], RING * r + n + 1)
                past(dve, s["fm1"], r, n - 1)
                dve.tensor_copy(xgT[:, n % 2, :], bank[n % 2][:, 0:P]).then_inc(s["fxc"], 1)

            def expert(r, n):
                return dve.value_load(tile_e[0:1, bass.ds(RING * r + n, 1)], min_val=0, max_val=E_ - 1)

            def add_b1(r, n):
                e = expert(r, n)
                dve.wait_ge(s["fm1"], RING * r + n + 1)
                past(dve, s["fge"], r, n - 1)
                dve.tensor_tensor(hs[:, n % 2, :], bank[2 + n % 2][:, :], b1s[:, bass.ds(e * F, F)], ALU.add)\
                    .then_inc(s["fad"], 1)

            def add_b2(r, n):
                e = expert(r, n)
                dve.wait_ge(s["fm2"], RING * r + n + 1)
                dve.tensor_tensor(ys[:, n % RING, :], bank[6 + n % 2][:, 0:P], b2s[:, bass.ds(e * P, P)], ALU.add)\
                    .then_inc(s["fy"], 1)

            tiles(dve, (gather_index, 4), (x_copy, 3), (add_b1, 2), (scatter_index, 0), (add_b2, 0))
            for n in range(4):
                dve.wait_ge(s["y_in"], 128)
                for k, Y in enumerate((Y1, Y2)):
                    for c in range(8 * n, 8 * n + 8):
                        if k:
                            dve.wait_ge(s["fin"], 16 * n + c - 8 * n + 1)
                        dve.scalar_tensor_tensor(X[:, c, :], Y[:, c, :], prob[:, k, c:c + 1], X[:, c, :],
                                                 ALU.mult, ALU.add).then_inc(s["fin"], 1)


def kernel(**inputs):
    import numpy as np
    import concourse.bacc as _bacc
    from concourse.bass_utils import run_bass_kernel_spmd as _run

    c = {k[8:]: np.asarray(v) for k, v in inputs.items() if k.startswith("L0_conv_")}
    names = ["l1", "g1", "l2", "g2", "g5", "l3", "g3", "l4", "g4", "l5"]
    arrays = {
        "x": np.asarray(inputs["x"]), "z2": c["z2"], "z3": c["z3"],
        "conv_w": np.stack([c[n + "_w"] for n in names], axis=1),
        "conv_b": np.stack([c[n + "_b"] for n in names]),
        "ln_p": np.stack([np.stack([c[f"ln{i}_w"], c[f"ln{i}_b"]], axis=1) for i in (1, 2, 3, 5)], axis=1),
    }
    for n in ("W_g", "w1", "b1", "w2", "b2"):
        arrays[n] = np.asarray(inputs["L0_ffn_" + n])
    nc = _bacc.Bacc("TRN2", target_bir_lowering=False, num_devices=1)
    feeds, args = {}, []
    for name, a in arrays.items():
        a = np.ascontiguousarray(a)
        feeds[f"in_{name}"] = a
        args.append(nc.dram_tensor(f"in_{name}", a.shape, mybir.dt.from_np(a.dtype), kind="ExternalInput").ap())
    args.append(nc.dram_tensor("out", (1, C, P, P), F32, kind="ExternalOutput").ap())
    build(nc, *args)
    r = _run(nc, [feeds], core_ids=[0])
    return r.results[0]["out"]
```

```python
from contextlib import ExitStack

import concourse.bass as bass
from concourse import mybir

ALU = mybir.AluOpType
ACT = mybir.ActivationFunctionType
F32 = mybir.dt.float32
BF16 = mybir.dt.bfloat16
I32 = mybir.dt.int32
AX = mybir.AxisListType

P = 128
C = 32
Q = P // C
CH = P // Q
NCH = 4
SLOTS = 10
GROUPS = [(0, 5), (5, 7), (7, 9), (9, 10)]
E_ = 8
F = 512
K_ = F // P
TOP = 2
TILES = 72
ROWS_ = TILES + 4
BODY = 8
RING = 4
EPS_C, EPS = 1e-6, 1e-5


def build(nc, x, z2, z3, conv_w, conv_b, ln_p, W_g, w1, b1, w2, b2, out):
    with ExitStack() as ctx:
        def sb(name, shape, dt=F32):
            return ctx.enter_context(nc.sbuf_tensor(name, shape, dt))

        def sem(name):
            return ctx.enter_context(nc.semaphore(name))

        bank = [ctx.enter_context(nc.psum_tensor(f"bank{i}", [P, 512], F32)) for i in range(8)]

        X = sb("X", [P, C, P])
        Z23 = sb("Z23", [P, 2, C, P])
        Z2, Z3 = Z23[:, 0], Z23[:, 1]
        ZA = sb("ZA", [P, C, P])
        ZB = sb("ZB", [P, C, P])
        ZD = sb("ZD", [P, P, C])
        p2T = sb("p2T", [P, C, P])
        p3T = sb("p3T", [P, C, P])
        z12, z13 = Z2, Z3
        R = sb("R", [P, SLOTS, Q, C])
        RS = sb("RS", [P, SLOTS, Q, C])
        lnp = sb("lnp", [P, 4, 2])
        lnb = sb("lnb", [P, 4, 96])
        braw = sb("braw", [96, SLOTS, C])
        ZDf = ZD[:].rearrange("p a b -> p (a b)")
        bsum = ZDf[0:96, 0:SLOTS * P].rearrange("p (s q c) -> p s q c", s=SLOTS, q=Q)
        bhi = ZDf[0:96, 2048:2048 + SLOTS * C * 2].bitcast(BF16)
        bmid = ZDf[0:96, 3072:3072 + SLOTS * C * 2].bitcast(BF16)
        BB = sb("BB", [96, SLOTS * P], BF16)
        pick3 = sb("pick3", [96, P], BF16)
        ident = sb("ident", [P, P])
        blk = sb("blk", [P, P])
        cen = sb("cen", [P, P])
        mhalf = sb("mhalf", [P, C])
        sq = sb("sq", [P, 2, 512])
        sd = sb("sd", [P, 2, 512])
        rn = sb("rn", [P, 2, 512])
        sg = sb("sg", [P, 2, 256])
        epsc = sb("epsc", [P, 1])
        bn = sb("bn", [P, C, 6])
        st = sb("st", [P, 8, C])
        mu = sb("mu", [P, P])
        var = sb("var", [P, P])
        rsd = sb("rsd", [P, P])
        um, ue = sq, sd

        Asq = ctx.enter_context(nc.sbuf_tensor("Asq", [P, 2, CH * C], F32))
        sig5 = ZA[:].rearrange("p a b -> p (a b)").rearrange("p (j c) -> p j c", c=C)
        Zt = ZB
        p3j = p3T[:].rearrange("p a b -> p (a b)").rearrange("p (j c) -> p j c", c=C)
        T5 = p2T

        w1s = Z2.rearrange("p c j -> p (c j)")
        w2s = Z3.rearrange("p c j -> p (c j)")
        b1r = sb("b1r", [E_ * K_, P])
        b1T = sb("b1T", [P, E_ * K_])
        b2s = sb("b2s", [P, E_ * P])
        XL = ZB
        XT = p2T
        BH = p3T[:].rearrange("p a b -> p (a b)").bitcast(BF16).rearrange("p (n b) -> p n b", b=P)
        AW = sb("AW", [P, TOP * C, 2, TILES], BF16)
        wg = sb("wg", [P, E_])
        ZAf = ZA[:].rearrange("p a b -> p (a b)")
        rt = ZAf[:, 0:12 * C * E_].rearrange("p (k n) -> p k n", k=12)
        te = ZAf[:, 12 * C * E_:12 * C * E_ + ROWS_ * E_].rearrange("p (t e) -> p t e", e=E_)
        rs_ = sb("rs_", [P, 10, C])
        re_ = sb("re_", [P, 8, E_])
        prob = sb("prob", [P, TOP, C])
        slot = sb("slot", [P, TOP, C])
        sloti = sb("sloti", [P, 3, TOP * C], I32)
        slota = sb("slota", [P, 2, TOP * C])
        M_ = sb("M_", [P, C * E_], BF16)
        lower = sb("lower", [P, P], BF16)
        ones = sb("ones", [P, P], BF16)
        iota_w = sb("iota_w", [P, P])
        iota_p = sb("iota_p", [P, 1])
        spare = sb("spare", [P, TILES])
        cnum = sb("cnum", [P, TOP * C])
        w8 = sb("w8", [P, E_])
        thr = sb("thr", [P, C])
        zero256 = sb("zero256", [P, C * E_])
        vt = sb("vt", [P, 6, TILES])
        idx = sb("idx", [P, TOP, TILES], I32)
        tef = sb("tef", [P, ROWS_])
        tile_e = sb("tile_e", [P, ROWS_], I32)
        gix = sb("gix", [P, RING, 1], I32)
        six = sb("six", [P, RING, 1], I32)
        XTf = XT[:].rearrange("p c i -> p (c i)")
        xg = XTf[:, 0:512].rearrange("p (n h) -> p n h", n=RING)
        xgT = XTf[:, 512:768].rearrange("p (n h) -> p n h", n=2)
        hs = XTf[:, 1024:2048].rearrange("p (n f) -> p n f", n=2)
        hg = XTf[:, 2048:3072].rearrange("p (n f) -> p n f", n=2)
        w1t = XTf[:, 3072:4096].rearrange("p (n f) -> p n f", n=2)
        ys = sb("ys", [P, RING, P])
        Y1, Y2 = p2T, p3T
        xrows = nc.dram_tensor("xrows", (C * P, P), F32)
        yrows = nc.dram_tensor("yrows", ((TOP * C + TILES) * P, P), F32)
        g_in = [sem(f"g_in{i}") for i in range(RING)]
        y_in = [sem(f"y_in{i}") for i in range(4)]
        sct = [sem(f"sct{i}") for i in range(RING)]

        s = {n: sem(n) for n in (
            "w_in xr_out tbn tst trs xln txl txlc lgt rt_ rex wk rank vmm ve idx_set te_set cst b1_in b1_turned b1_set "
            "ftx fxc fw1 fm1 fad fge fm2 fy fsi fgi pool_go fin").split()}
        s |= {n: sem(n) for n in (
            "wts_in ones_set r_zero diag_in lnp_in braw_in x_in z2_in z3_in "
            "consts lnb_set bias_mm bsum_set b_step bb_set rs_set mh_set "
            "cen2 sq2 var2 sd2 rn2 zn2 cen3 sq3 var3 sd3 rn3 zn3 "
            "pr2 sg2 gate2 pr3 sg3 gate3 "
            "xbn xst xrs z1 amu acen asq avar ars anorm "
            "t1 t1c pra sga gata g5mm g5s tz tzc ein einc "
            "mu5 cen5 sq5 var5 rs5 norm5 t5 t5c pr5 u5 um5 ue5 y5 x2 out_done").split()}

        block = ctx.enter_context(nc.Block())
        x_v = x.rearrange("a c i j -> i (a c) j")
        out_v = out.rearrange("a c i j -> i (a c) j")

        def rsqrt(act, out, v, ready, count, done, before):
            act.preload_act_table_set("natural_log_exp_and_others")
            act.wait_ge(s[ready], count)
            act.activation(out, v, ACT.Ln).then_inc(s[done], 1)
            act.wait_ge(s[done], before + 1)
            act.activation(out, out, ACT.Exp, scale=-0.5).then_inc(s[done], 1)

        def elu_exp(act, n):
            act.wait_ge(s["um5"], n + 1)
            if n >= 2:
                act.wait_ge(s["y5"], n - 1)
            act.activation(ue[:, n % 2, :], um[:, n % 2, :], ACT.Exp).then_inc(s["ue5"], 1)

        def elu_add(dve, n):
            U = sig5[:, 16 * n:16 * n + 16, :].rearrange("p j c -> p (j c)")
            dve.wait_ge(s["ue5"], n + 1)
            dve.scalar_tensor_tensor(U, ue[:, n % 2, :], -1.0, U, ALU.add, ALU.max).then_inc(s["y5"], 1)
            dve.wait_ge(s["y5"], n + 1)
            xs = X[:, :, 16 * n:16 * n + 16].rearrange("p c j -> p j c")
            dve.tensor_tensor(xs, xs, sig5[:, 16 * n:16 * n + 16, :], ALU.add).then_inc(s["x2"], 1)

        def row_stats(dve, eps, tag, base):
            me, mo, ve, vo = bn[:, :, 1], bn[:, :, 4], bn[:, :, 2], bn[:, :, 5]
            dve.tensor_tensor(st[:, 0, :], me, mo, ALU.add).then_inc(s[tag], 1)
            dve.tensor_tensor(st[:, 1, :], me, mo, ALU.subtract).then_inc(s[tag], 1)
            dve.tensor_tensor(st[:, 3, :], ve, vo, ALU.add).then_inc(s[tag], 1)
            dve.wait_ge(s[tag], base + 3)
            dve.tensor_scalar(st[:, 2, :], st[:, 0, :], 0.5, None, ALU.mult)
            dve.scalar_tensor_tensor(st[:, 4, :], st[:, 1, :], 0.25, st[:, 1, :], ALU.mult, ALU.mult)\
                .then_inc(s[tag], 1)
            dve.tensor_scalar(st[:, 7, :], st[:, 3, :], 1.0 / P, eps, ALU.mult, ALU.add).then_inc(s[tag], 1)
            dve.wait_ge(s[tag], base + 5)
            dve.tensor_tensor(st[:, 5, :], st[:, 7, :], st[:, 4, :], ALU.add).then_inc(s[tag], 1)

        def past(eng, signal, r, n):
            if not isinstance(r, int) or BODY * r + n > 0:
                eng.wait_ge(signal, BODY * r + n)

        expert_of = {}

        def load_experts(eng, r, quad):
            _, vals = nc.values_load_multi_w_load_instructions(
                tile_e[0:1, bass.ds(BODY * r + 4 * quad, 4)], engines=(eng.engine,), min_val=0, max_val=E_ - 1,
                skip_runtime_bounds_check_because="the table's entries are a count of 0 to 8, cut at 7")
            for n, v in enumerate(vals):
                expert_of[4 * quad + n] = v

        def tiles(eng, experts, *stages):
            def body(r, first):
                for n in range(first, BODY):
                    if experts and n == 0:
                        load_experts(eng, r, 0)
                    if experts and n >= 0 and n % 4 == 1:
                        load_experts(eng, r, n // 4 + 1)
                    for stage, ahead in stages:
                        if not isinstance(r, int) or 0 <= BODY * r + n + ahead < TILES:
                            stage(r, n + ahead)
            if experts:
                load_experts(eng, 0, 0)
            body(0, -7)
            with eng.Fori(1, TILES // BODY - 1) as r:
                body(r, 0)
            body(TILES // BODY - 1, 0)

        def logits(pe, n):
            pe.wait_ge(s["txlc"], n + 1)
            for c in range(4 * n, 4 * n + 4):
                mm = pe.matmul(bank[6][:, c * E_:(c + 1) * E_], XT[:, c, :], wg[:], start=True, stop=True)
            mm.then_inc(s["lgt"], 1)

        @block.sync
        def _(sp):
            sp.wait_ge(s["r_zero"], 1)
            for q in range(Q):
                sp.dma_start(R[q * C:(q + 1) * C, :, q, :], conv_w).then_inc(s["diag_in"], 16)
            for q in range(Q):
                sp.dma_start(lnp[q * C:(q + 1) * C, :, :], ln_p).then_inc(s["lnp_in"], 16)
            sp.dma_start(braw[:, :, :], conv_b.partition_broadcast(96)).then_inc(s["braw_in"], 16)
            for q in range(Q):
                sp.dma_start(Z2[q * C:(q + 1) * C, :, :], z2[0, :, q * C:(q + 1) * C, :]).then_inc(s["z2_in"], 16)
            sp.dma_start(X[:, :, :], x_v).then_inc(s["x_in"], 16)
            for q in range(Q):
                sp.dma_start(Z3[q * C:(q + 1) * C, :, :], z3[0, :, q * C:(q + 1) * C, :]).then_inc(s["z3_in"], 16)
            sp.dma_start(b1r[:], b1.rearrange("e (k f) -> (e k) f", k=K_)).then_inc(s["b1_in"], 16)
            sp.dma_start(wg[:], W_g).then_inc(s["w_in"], 16)
            sp.dma_start(b2s[:], b2.rearrange("e h -> (e h)").partition_broadcast(P)).then_inc(s["w_in"], 16)
            sp.wait_ge(s["ein"], 8)
            sp.dma_start(w1s.rearrange("p (e f) -> p e f", e=E_), w1.rearrange("e h f -> h e f")).then_inc(s["w_in"], 16)
            sp.dma_start(w2s.rearrange("p (e k h) -> p e k h", e=E_, h=P), w2.rearrange("e (k p) h -> p e k h", p=P))\
                .then_inc(s["w_in"], 16)
            xr = xrows.ap().rearrange("(c i) j -> i c j", i=P)
            for n in range(4):
                sp.wait_ge(s["xln"], 8 * n + 8)
                sp.dma_start(xr[:, 8 * n:8 * n + 8, :], XL[:, 8 * n:8 * n + 8, :]).then_inc(s["xr_out"], 16)
            for u in range(RING):
                sp.wait_ge(sct[u], 16 * (TILES // RING))
            yr = yrows.ap()[0:TOP * C * P, :].rearrange("(k c i) j -> k i c j", k=TOP, i=P)
            for n in range(4):
                for k, Y in enumerate((Y1, Y2)):
                    sp.dma_start(Y[:, 8 * n:8 * n + 8, :], yr[k][:, 8 * n:8 * n + 8, :]).then_inc(y_in[n], 16)
            for n in range(4):
                sp.wait_ge(s["fin"], 16 * (n + 1))
                sp.dma_start(out_v[:, 8 * n:8 * n + 8, :], X[:, 8 * n:8 * n + 8, :]).then_inc(s["out_done"], 16)
            sp.wait_ge(s["out_done"], 64)

        @block.gpsimd
        def _(pool):
            pool.memset(R[:], 0.0).then_inc(s["r_zero"], 1)
            pool.memset(ident[:], 0.0).then_inc(s["ones_set"], 1)
            pool.wait_ge(s["ones_set"], 1)
            pool.affine_select(out=ident[:], in_=ident[:], compare_op=ALU.not_equal, fill=1.0, base=0,
                               pattern=[[-1, P]], channel_multiplier=1).then_inc(s["ones_set"], 1)
            pool.memset(lower[:], 1.0).then_inc(s["cst"], 1)
            pool.wait_ge(s["cst"], 1)
            pool.affine_select(out=lower[:], in_=lower[:], compare_op=ALU.is_gt, fill=0.0, base=0,
                               pattern=[[1, P]], channel_multiplier=-1).then_inc(s["cst"], 1)
            imp = dict(allow_small_or_imprecise_dtypes=True)
            pool.iota(iota_w[:], pattern=[[1, P]], base=0, channel_multiplier=0, **imp).then_inc(s["cst"], 1)
            pool.iota(iota_p[:], pattern=[[0, 1]], base=0, channel_multiplier=1, **imp).then_inc(s["cst"], 1)
            pool.iota(spare[:], pattern=[[P, TILES]], base=(TOP * C + 1) * P, channel_multiplier=1, **imp)\
                .then_inc(s["cst"], 1)
            pool.iota(cnum[:], pattern=[[1, TOP * C]], base=1, channel_multiplier=0, **imp).then_inc(s["cst"], 1)
            pool.iota(w8[:], pattern=[[-1, E_]], base=E_, channel_multiplier=0, **imp).then_inc(s["cst"], 1)
            pool.iota(thr[:], pattern=[[P, C]], base=0, channel_multiplier=0, **imp).then_inc(s["cst"], 1)
            def gather(r, n):
                pool.wait_ge(s["fgi"], BODY * r + n + 1)
                past(pool, s["ftx"], r, n - RING + 1)
                pool.sem_inc(s["pool_go"], 1)
                pool.indirect_dma_start(out=xg[:, n % RING, :], out_offset=None, in_=xrows.ap(),
                                        in_offset=bass.IndirectOffsetOnAxis(ap=gix[:, n % RING, :], axis=0))\
                    .then_inc(g_in[n % RING], 16)

            def scatter(r, n):
                pool.wait_ge(s["fsi"], BODY * r + n + 1)
                pool.wait_ge(s["fy"], BODY * r + n + 1)
                pool.sem_inc(s["pool_go"], 1)
                pool.indirect_dma_start(out=yrows.ap(), in_=ys[:, n % RING, :], in_offset=None,
                                        out_offset=bass.IndirectOffsetOnAxis(ap=six[:, n % RING, :], axis=0))\
                    .then_inc(sct[n % RING], 16)

            pool.wait_ge(s["xr_out"], 64)
            tiles(pool, False, (gather, 5), (scatter, 0))

        @block.tensor
        def _(pe):
            pe.wait_ge(s["diag_in"], 64)
            pe.wait_ge(s["lnb_set"], 4)
            for n, (g, a, b, bk) in enumerate([(0, 0, 4, 0), (0, 4, 5, 1), (1, 5, 7, 2), (2, 7, 9, 3), (3, 9, 10, 4)]):
                pe.matmul(bank[bk][0:96, 0:(b - a) * P], lnb[:, g, :], R[:, a:b].rearrange("p s q c -> p (s q c)"),
                          start=True, stop=True).then_inc(s["bias_mm"], 1)

            def norm(zin, z, tag):
                pe.wait_ge(s["consts"], 1)
                pe.wait_ge(s[zin], 64)

                def centre(n):
                    if n >= 2:
                        pe.wait_ge(s["zn" + tag], n - 1)
                    pe.matmul(bank[n % 2][:, :], cen[:], z[:, 4 * n:4 * n + 4, :].rearrange("p i j -> p (i j)"),
                              start=True, stop=True).then_inc(s["cen" + tag], 1)
                centre(0)
                for n in range(8):
                    if n < 7:
                        centre(n + 1)
                    pe.wait_ge(s["sq" + tag], n + 1)
                    if n >= 2:
                        pe.wait_ge(s["sd" + tag], n - 1)
                    pe.matmul(bank[2 + n % 2][:, :], blk[:], sq[:, n % 2, :], start=True, stop=True)\
                        .then_inc(s["var" + tag], 1)

            def proj(z, tag, a, m, before):
                if before + m >= 4:
                    pe.wait_ge(s["gate2"], min(16, before + m - 3))
                    if before + m - 3 > 16:
                        pe.wait_ge(s["gate3"], before + m - 3 - 16)
                pe.wait_ge(s["zn" + tag], m // 2 + 1)
                pe.wait_ge(s["bb_set"], 3)
                pe.wait_ge(s["rs_set"], 4)
                for h in range(2):
                    o = bank[4 + m % 4][:, 256 * h:256 * h + 256]
                    pe.matmul(o, z[:, 2 * m + h, :], RS[:, a:a + 2].rearrange("p s q c -> p (s q c)"),
                              start=True, stop=False)
                    mm = pe.matmul(o, pick3[:], BB[:, a * P:(a + 2) * P], start=False, stop=True)
                mm.then_inc(s["pr" + tag], 1)

            pe.wait_ge(s["bsum_set"], 5)
            norm("z2_in", Z2, "2")
            for m in range(16):
                proj(Z2, "2", 5, m, 0)
            norm("z3_in", Z3, "3")

            def t1(k):
                pe.wait_ge(s["anorm"], k + 1)
                for h in range(2):
                    n = 2 * k + h
                    if n >= 2:
                        pe.wait_ge(s["t1c"], n - 1)
                    else:
                        pe.wait_ge(s["zn3"], 8)
                    for v in range(4):
                        j0 = (4 * n + v) * 4
                        mm = pe.transpose(bank[n % 2][:, v * P:(v + 1) * P],
                                          ZD[:, j0:j0 + 4, :].rearrange("p j c -> p (j c)"), ident[:])
                    mm.then_inc(s["t1"], 1)
            for m in range(16):
                proj(Z3, "3", 7, m, 16)
            for k in range(NCH):
                t1(k)
            pe.wait_ge(s["b1_in"], 16)
            pe.wait_ge(s["t1c"], 7)
            pe.transpose(bank[0][:, 0:E_ * K_], b1r[:], ident[0:E_ * K_, 0:E_ * K_]).then_inc(s["b1_turned"], 1)
            for n in range(C):
                pe.wait_ge(s["t1c"], n // 4 + 1)
                if n >= 4:
                    pe.wait_ge(s["gata"], n - 3)
                else:
                    pe.wait_ge(s["gate3"], 13 + n)
                pe.matmul(bank[4 + n % 4][:, :], ZB[:, n, :], RS[:, 0:4].rearrange("p s q c -> p (s q c)"),
                          start=True, stop=False)
                pe.matmul(bank[4 + n % 4][:, :], pick3[:], BB[:, 0:512], start=False, stop=True)\
                    .then_inc(s["pra"], 1)
                g = n // 4
                if n % 4 == 0:
                    if g >= 2:
                        pe.wait_ge(s["g5s"], g - 1)
                    else:
                        pe.wait_ge(s["zn3"], 8)
                o = bank[2 + g % 2][:, (n % 4) * P:(n % 4 + 1) * P]
                pe.matmul(o, ZB[:, n, :], RS[:, 4].rearrange("p q c -> p (q c)"), start=True, stop=False)
                mm = pe.matmul(o, pick3[:], BB[:, 512:640], start=False, stop=True)
                if n % 4 == 3:
                    mm.then_inc(s["g5mm"], 1)
            pe.wait_ge(s["gata"], C)
            for n in range(8):
                pe.wait_ge(s["tzc"] if n >= 2 else s["b1_set"], n - 1 if n >= 2 else 1)
                for v in range(4):
                    mm = pe.transpose(bank[n % 2][:, v * P:(v + 1) * P], z13[:, 4 * n + v, :], ident[:])
                mm.then_inc(s["tz"], 1)
            pe.wait_ge(s["tzc"], 8)
            for n in range(8):
                if n >= 4:
                    pe.wait_ge(s["einc"], n - 3)
                d = slice(64 * (n // 4), 64 * (n // 4) + 64)
                for v in range(8):
                    c = 8 * (n % 4) + v
                    o = bank[4 + n % 4][:, v * 64:(v + 1) * 64]
                    pe.matmul(o, p2T[:, c, :], z12[:, c, d], start=True, stop=False)
                    mm = pe.matmul(o, ZDf[:, c * P:(c + 1) * P], p3T[:, c, d], start=False, stop=True)
                mm.then_inc(s["ein"], 1)
            def t5(n):
                pe.wait_ge(s["norm5"], n // 2 + 1)
                if n >= 2:
                    pe.wait_ge(s["t5c"], n - 1)
                for v in range(4):
                    j0 = (4 * n + v) * 4
                    mm = pe.transpose(bank[n % 2][:, v * P:(v + 1) * P],
                                      p3j[:, j0:j0 + 4, :].rearrange("p j c -> p (j c)"), ident[:])
                mm.then_inc(s["t5"], 1)
            t5(0)
            for n in range(8):
                if n < 7:
                    t5(n + 1)
                pe.wait_ge(s["t5c"], n + 1)
                if n >= 2:
                    pe.wait_ge(s["u5"], n - 1)
                for v in range(4):
                    o = bank[2 + n % 2][:, v * P:(v + 1) * P]
                    pe.matmul(o, T5[:, 4 * n + v, :], RS[:, 9].rearrange("p q c -> p (q c)"), start=True, stop=False)
                    mm = pe.matmul(o, pick3[:], BB[:, 9 * P:10 * P], start=False, stop=True)
                mm.then_inc(s["pr5"], 1)
            for n in range(8):
                pe.wait_ge(s["xln"], 4 * n + 4)
                if n >= 2:
                    pe.wait_ge(s["txlc"], n - 1)
                for v in range(4):
                    mm = pe.transpose(bank[4 + n % 2][:, v * P:(v + 1) * P], XL[:, 4 * n + v, :], ident[:])
                mm.then_inc(s["txl"], 1)
                if n == 0:
                    pe.wait_ge(s["w_in"], 64)
                else:
                    logits(pe, n - 1)
            logits(pe, 7)
            pe.wait_ge(s["wk"], 1)
            pe.wait_ge(s["mh_set"], 14)
            pe.matmul(bank[7][:, 0:256], lower[:], M_[:], start=True, stop=True)
            pe.matmul(bank[7][:, 256:512], ones[:], M_[:], start=True, stop=True).then_inc(s["rank"], 1)
            pe.wait_ge(s["vmm"], 4)
            for n in range(TOP * C):
                mm = pe.matmul(bank[0][:, 0:2 * TILES], BH[:, n, :], AW[:, n].rearrange("p t a -> p (t a)"),
                               start=(n == 0), stop=(n == TOP * C - 1))
            mm.then_inc(s["ve"], 1)
            pe.wait_ge(s["te_set"], 5)

            def x_turn(r, n):
                pe.wait_ge(g_in[n % RING], 16 * (BODY // RING * r + n // RING + 1))
                past(pe, s["fxc"], r, n - 1)
                pe.transpose(bank[n % 2][:, 0:P], xg[:, n % RING, :], ident[:]).then_inc(s["ftx"], 1)

            def up(r, n):
                pe.wait_ge(s["fxc"], BODY * r + n + 1)
                past(pe, s["fad"], r, n - 1)
                pe.wait_ge(s["fw1"], BODY * r + n + 1)
                for k in range(K_):
                    mm = pe.matmul(bank[2 + n % 2][:, k * P:(k + 1) * P], w1t[:, n % 2, k * P:(k + 1) * P],
                                   xgT[:, n % 2, :], start=True, stop=True)
                mm.then_inc(s["fm1"], 1)

            def down(r, n):
                e = expert_of[n]
                pe.wait_ge(s["fge"], BODY * r + n + 1)
                past(pe, s["fy"], r, n - 1)
                for k in range(K_):
                    mm = pe.matmul(bank[6 + n % 2][:, 0:P], hg[:, n % 2, k * P:(k + 1) * P],
                                   w2s[:, bass.ds(e * F + k * P, P)], start=(k == 0), stop=(k == K_ - 1))
                mm.then_inc(s["fm2"], 1)

            tiles(pe, True, (x_turn, 2), (up, 1), (down, 0))

        @block.scalar
        def _(act):
            def norm(tag):
                act.preload_act_table_set("natural_log_exp_and_others")
                act.wait_ge(s["mh_set"], 7)

                def square(n):
                    act.wait_ge(s["cen" + tag], n + 1)
                    if n >= 2:
                        act.wait_ge(s["var" + tag], n - 1)
                    act.activation(sq[:, n % 2, :], bank[n % 2][:, :], ACT.Square).then_inc(s["sq" + tag], 1)
                square(0)
                for n in range(8):
                    if n < 7:
                        square(n + 1)
                    act.wait_ge(s["var" + tag], n + 1)
                    if n >= 2:
                        act.wait_ge(s["zn" + tag], n - 1)
                    act.activation(sd[:, n % 2, :], bank[2 + n % 2][:, :], ACT.Ln, bias=epsc[:, 0:1])\
                        .then_inc(s["sd" + tag], 1)
                    act.wait_ge(s["sd" + tag], n + 1)
                    act.activation(rn[:, n % 2, :], sd[:, n % 2, :], ACT.Exp, scale=-0.5).then_inc(s["rn" + tag], 1)

            def sigma(tag, m, before):
                act.wait_ge(s["pr" + tag], m + 1)
                if m >= 2:
                    act.wait_ge(s["gate" + tag], m - 1)
                elif before:
                    act.wait_ge(s["gate2"], 15 + m)
                act.activation(sg[:, m % 2, :].rearrange("p (h n) -> p h n", h=2),
                               bank[4 + m % 4][:].rearrange("p (h t n) -> p h t n", h=2, t=2)[:, :, 1, :],
                               ACT.Sigmoid).then_inc(s["sg" + tag], 1)

            norm("2")
            for m in range(16):
                sigma("2", m, 0)
            rsqrt(act, st[:, 6, :], st[:, 5, :], "xst", 6, "xrs", 0)
            norm("3")

            def t1_copy(n):
                act.wait_ge(s["t1"], n + 1)
                act.activation(ZB[:, 4 * n:4 * n + 4, :].rearrange("p a b -> p (a b)"), bank[n % 2][:, :], ACT.Copy)\
                    .then_inc(s["t1c"], 1)
            for m in range(16):
                sigma("3", m, 16)
                if 5 <= m < 9:
                    k = m - 5
                    act.wait_ge(s["acen"], k + 1)
                    act.activation(ZB[:].rearrange("p a b -> p (a b)")[:, k * CH * C:(k + 1) * CH * C],
                                   ZA[:, :, k * CH:(k + 1) * CH].rearrange("p c j -> p j c"), ACT.Square)\
                        .then_inc(s["asq"], 1)
                if m == 11:
                    rsqrt(act, rsd[:], var[:], "avar", 8, "ars", 0)
            for n in range(8):
                t1_copy(n)
            act.wait_ge(s["b1_turned"], 1)
            act.activation(b1T[:], bank[0][:, 0:E_ * K_], ACT.Copy).then_inc(s["b1_set"], 1)
            for n in range(C):
                act.wait_ge(s["pra"], n + 1)
                if n >= 2:
                    act.wait_ge(s["gata"], n - 1)
                else:
                    act.wait_ge(s["gate3"], 15 + n)
                act.activation(sg[:, n % 2, :].rearrange("p (h n) -> p h n", h=2),
                               bank[4 + n % 4][:].rearrange("p (h t n) -> p h t n", h=2, t=2)[:, :, 1, :],
                               ACT.Sigmoid).then_inc(s["sga"], 1)
                if n % 4 == 3:
                    g = n // 4
                    act.wait_ge(s["g5mm"], g + 1)
                    act.activation(sig5[:, 16 * g:16 * g + 16, :].rearrange("p j c -> p (j c)"),
                                   bank[2 + g % 2][:, :], ACT.Sigmoid).then_inc(s["g5s"], 1)
            for n in range(8):
                act.wait_ge(s["tz"], n + 1)
                act.activation(ZD[:].rearrange("p a b -> p (a b)")[:, 512 * n:512 * n + 512], bank[n % 2][:, :],
                               ACT.Copy).then_inc(s["tzc"], 1)
            def z_copy(n):
                act.wait_ge(s["ein"], n + 1)
                act.activation(Zt[:, 8 * (n % 4):8 * (n % 4) + 8, 64 * (n // 4):64 * (n // 4) + 64],
                               bank[4 + n % 4][:, :].rearrange("p (c j) -> p c j", c=8), ACT.Copy).then_inc(s["einc"], 1)

            def squares5(k):
                act.wait_ge(s["cen5"], k + 1)
                if k >= 2:
                    act.wait_ge(s["var5"], 2 * k - 2)
                act.activation(Asq[:, k % 2, :].rearrange("p (j c) -> p j c", c=C),
                               Zt[:, :, k * CH:(k + 1) * CH].rearrange("p c j -> p j c"), ACT.Square)\
                    .then_inc(s["sq5"], 1)
            for n in range(8):
                z_copy(n)
            for h in range(2):
                squares5(2 * h)
                squares5(2 * h + 1)
                rsqrt(act, rsd[:, 64 * h:64 * h + 64], var[:, 64 * h:64 * h + 64], "var5", 4 * h + 4, "rs5", 2 * h)
            for n in range(8):
                act.wait_ge(s["t5"], n + 1)
                act.activation(T5[:, 4 * n:4 * n + 4, :].rearrange("p a b -> p (a b)"), bank[n % 2][:, :],
                               ACT.Copy).then_inc(s["t5c"], 1)
                if n:
                    elu_exp(act, n - 1)
            elu_exp(act, 7)
            rsqrt(act, st[:, 6, :], st[:, 5, :], "tst", 6, "trs", 0)
            for n in range(8):
                act.wait_ge(s["txl"], n + 1)
                act.activation(XT[:, 4 * n:4 * n + 4, :].rearrange("p a b -> p (a b)"), bank[4 + n % 2][:, :],
                               ACT.Copy).then_inc(s["txlc"], 1)
            act.wait_ge(s["rt_"], 2)
            act.activation(rt[:, 1, :], rt[:, 0, :], ACT.Exp).then_inc(s["rex"], 1)
            act.wait_ge(s["te_set"], 5)
            act.wait_ge(s["w_in"], 64)

            def gelu(r, n):
                act.wait_ge(s["fad"], BODY * r + n + 1)
                past(act, s["fm2"], r, n - 1)
                act.activation(hg[:, n % 2, :], hs[:, n % 2, :], ACT.Gelu).then_inc(s["fge"], 1)

            def w1_copy(r, n):
                e = expert_of[n]
                past(act, s["fm1"], r, n - 1)
                act.activation(w1t[:, n % 2, :], w1s[:, bass.ds(e * F, F)], ACT.Copy).then_inc(s["fw1"], 1)

            tiles(act, True, (w1_copy, 2), (gelu, 1))

        @block.vector
        def _(dve):
            dve.memset(mhalf[:], -0.5).then_inc(s["mh_set"], 1)
            dve.memset(pick3[:], 0.0).then_inc(s["mh_set"], 1)
            dve.memset(epsc[:], EPS).then_inc(s["mh_set"], 1)
            dve.memset(BB[:], 0.0).then_inc(s["mh_set"], 1)
            dve.memset(ones[:], 1.0).then_inc(s["mh_set"], 1)
            dve.memset(zero256[:], 0.0).then_inc(s["mh_set"], 1)
            dve.memset(blk[:], 0.0).then_inc(s["mh_set"], 1)
            dve.wait_ge(s["mh_set"], 7)
            for k in range(3):
                dve.memset(pick3[32 * k:32 * k + 1, :], 1.0).then_inc(s["mh_set"], 1)
            for q in range(Q):
                d = slice(q * C, (q + 1) * C)
                dve.memset(blk[d, d], 1.0 / C).then_inc(s["mh_set"], 1)
            dve.wait_ge(s["ones_set"], 2)
            dve.wait_ge(s["mh_set"], 10 + Q)
            dve.tensor_tensor(cen[:], ident[:], blk[:], ALU.subtract).then_inc(s["consts"], 1)
            dve.wait_ge(s["lnp_in"], 64)
            for g in range(4):
                dve.tensor_copy(lnb[:, g, :], lnp[:, g, 1:2].to_broadcast([P, 96])).then_inc(s["lnb_set"], 1)
            dve.wait_ge(s["diag_in"], 64)
            for g, (a, b) in enumerate(GROUPS):
                dve.tensor_scalar(RS[:, a:b], R[:, a:b], lnp[:, g, 0:1], None, ALU.mult).then_inc(s["rs_set"], 1)
            dve.wait_ge(s["braw_in"], 16)
            for n, (a, b, bk) in enumerate([(0, 4, 0), (4, 5, 1), (5, 7, 2), (7, 9, 3), (9, 10, 4)]):
                dve.wait_ge(s["bias_mm"], n + 1)
                dve.tensor_tensor(bsum[:, a:b], bank[bk][0:96, 0:(b - a) * P].rearrange("p (s q c) -> p s q c", q=Q, c=C),
                                  braw[:, a:b].unsqueeze(2).to_broadcast([96, b - a, Q, C]), ALU.add)\
                    .then_inc(s["bsum_set"], 1)
            dve.wait_ge(s["bsum_set"], 5)
            bs = bsum[:].rearrange("p s q c -> p (s q c)")
            dve.tensor_copy(bhi[:], bs).then_inc(s["b_step"], 1)
            dve.wait_ge(s["b_step"], 1)
            dve.tensor_tensor(bs, bs, bhi[:], ALU.subtract).then_inc(s["b_step"], 1)
            dve.wait_ge(s["b_step"], 2)
            dve.tensor_copy(bmid[:], bs).then_inc(s["b_step"], 1)
            dve.wait_ge(s["b_step"], 3)
            dve.tensor_tensor(bs, bs, bmid[:], ALU.subtract).then_inc(s["b_step"], 1)
            dve.wait_ge(s["mh_set"], 7)
            dve.wait_ge(s["b_step"], 4)
            dve.tensor_copy(BB[0:1, :], bhi[0:1, :]).then_inc(s["bb_set"], 1)
            dve.tensor_copy(BB[32:33, :], bmid[32:33, :]).then_inc(s["bb_set"], 1)
            dve.tensor_copy(BB[64:65, :], bs[64:65, :]).then_inc(s["bb_set"], 1)

            def norm(z, tag, n):
                dve.wait_ge(s["rn" + tag], n + 1)
                dve.tensor_tensor(z[:, 4 * n:4 * n + 4, :].rearrange("p i j -> p (i j)"), bank[n % 2][:, :],
                                  rn[:, n % 2, :], ALU.mult).then_inc(s["zn" + tag], 1)

            def gate(dst, tag, m):
                dve.wait_ge(s["sg" + tag], m + 1)
                for h in range(2):
                    ins = dve.tensor_tensor(
                        dst[:].rearrange("p c (q i) -> p i q c", q=Q)[:, 2 * m + h],
                        bank[4 + m % 4][:, 256 * h:256 * h + P].rearrange("p (q c) -> p q c", q=Q),
                        sg[:, m % 2, h * P:(h + 1) * P].rearrange("p (q c) -> p q c", q=Q), ALU.mult)
                ins.then_inc(s["gate" + tag], 1)

            for n in range(8):
                norm(Z2, "2", n)
            dve.wait_ge(s["x_in"], 16)
            for m in range(16):
                gate(p2T, "2", m)
                for c in (2 * m, 2 * m + 1):
                    dve.bn_stats(bn[:, c, :], X[:, c, :]).then_inc(s["xbn"], 1)
            dve.wait_ge(s["xbn"], C)
            row_stats(dve, EPS_C, "xst", 0)
            for n in range(8):
                norm(Z3, "3", n)
                if n == 0:
                    dve.wait_ge(s["xrs"], 2)
                for c in range(4 * n, 4 * n + 4):
                    dve.tensor_scalar(ZA[:, c, :], X[:, c, :], st[:, 2, c:c + 1], st[:, 6, c:c + 1],
                                      ALU.subtract, ALU.mult).then_inc(s["z1"], 1)

            def channel_mean(src, k, tag):
                d = slice(k * CH, (k + 1) * CH)
                dve.tensor_reduce(mu[:, d], src[:, :, d].rearrange("p c j -> p j c"), AX.X, ALU.add)\
                    .then_inc(s[tag], 1)
                dve.wait_ge(s[tag], 2 * k + 1)
                dve.tensor_scalar(mu[:, d], mu[:, d], 1.0 / C, None, ALU.mult).then_inc(s[tag], 1)

            def channel_centre(src, k, tag_mu, tag):
                d = slice(k * CH, (k + 1) * CH)
                dve.wait_ge(s[tag_mu], 2 * k + 2)
                dve.tensor_tensor(src[:, :, d], src[:, :, d], mu[:, d].unsqueeze(1).to_broadcast([P, C, CH]),
                                  ALU.subtract).then_inc(s[tag], 1)

            def channel_var(sq, k, tag_sq, tag):
                d = slice(k * CH, (k + 1) * CH)
                dve.wait_ge(s[tag_sq], k + 1)
                dve.tensor_reduce(var[:, d], sq.rearrange("p (j c) -> p j c", c=C), AX.X, ALU.add)\
                    .then_inc(s[tag], 1)
                dve.wait_ge(s[tag], 2 * k + 1)
                dve.tensor_scalar(var[:, d], var[:, d], 1.0 / C, EPS, ALU.mult, ALU.add).then_inc(s[tag], 1)

            def channel_norm(dst, src, k, tag_rs, count, tag):
                d = slice(k * CH, (k + 1) * CH)
                dve.wait_ge(s[tag_rs], count)
                dve.tensor_tensor(dst[:, d, :], src[:, :, d].rearrange("p c j -> p j c"),
                                  rsd[:, d].unsqueeze(2).to_broadcast([P, CH, C]), ALU.mult).then_inc(s[tag], 1)

            dve.wait_ge(s["z1"], C)
            for m in range(16):
                gate(p3T, "3", m)
                k = m % 4
                if m < 4:
                    channel_mean(ZA, k, "amu")
                elif m < 8:
                    channel_centre(ZA, k, "amu", "acen")
                elif m < 12:
                    channel_var(ZB[:].rearrange("p a b -> p (a b)")[:, k * CH * C:(k + 1) * CH * C], k, "asq", "avar")
                else:
                    channel_norm(ZD, ZA, k, "ars", 2, "anorm")
            for n in range(C):
                dve.wait_ge(s["sga"], n + 1)
                for h in range(2):
                    ins = dve.tensor_tensor(
                        Z23[:, h, :, 4 * n:4 * n + 4].rearrange("p c j -> p j c"),
                        bank[4 + n % 4][:, 256 * h:256 * h + P].rearrange("p (j c) -> p j c", c=C),
                        sg[:, n % 2, h * P:(h + 1) * P].rearrange("p (j c) -> p j c", c=C), ALU.mult)
                ins.then_inc(s["gata"], 1)
            for h in range(2):
                dve.wait_ge(s["einc"], 4 * h + 4)
                for k in (2 * h, 2 * h + 1):
                    channel_mean(Zt, k, "mu5")
                for k in (2 * h, 2 * h + 1):
                    channel_centre(Zt, k, "mu5", "cen5")
                for k in (2 * h, 2 * h + 1):
                    channel_var(Asq[:, k % 2, :], k, "sq5", "var5")
                for k in (2 * h, 2 * h + 1):
                    channel_norm(p3j, Zt, k, "rs5", 2 * h + 2, "norm5")
            for n in range(8):
                dve.wait_ge(s["pr5"], n + 1)
                if n >= 2:
                    dve.wait_ge(s["ue5"], n - 1)
                dve.wait_ge(s["g5s"], 8)
                U = sig5[:, 16 * n:16 * n + 16, :].rearrange("p j c -> p (j c)")
                dve.tensor_tensor(U, bank[2 + n % 2][:, :], U, ALU.mult).then_inc(s["u5"], 1)
                dve.wait_ge(s["u5"], n + 1)
                dve.tensor_scalar(um[:, n % 2, :], U, 0.0, None, ALU.min).then_inc(s["um5"], 1)
                if n:
                    elu_add(dve, n - 1)
            elu_add(dve, 7)
            dve.wait_ge(s["x2"], 8)
            for c in range(C):
                dve.bn_stats(bn[:, c, :], X[:, c, :]).then_inc(s["tbn"], 1)
            dve.wait_ge(s["tbn"], C)
            row_stats(dve, EPS, "tst", 0)
            dve.wait_ge(s["trs"], 2)
            for c in range(C):
                dve.tensor_scalar(XL[:, c, :], X[:, c, :], st[:, 2, c:c + 1], st[:, 6, c:c + 1],
                                  ALU.subtract, ALU.mult).then_inc(s["xln"], 1)
            done = [0]

            def step(ins):
                ins.then_inc(s["rt_"], 1)
                done[0] += 1
                dve.wait_ge(s["rt_"], done[0])

            def ce(k):
                return rt[:, k, :].rearrange("p (c e) -> p c e", e=E_)

            def over_e(v):
                return v.unsqueeze(2).to_broadcast([P, C, E_])

            def over_c(v):
                return v.unsqueeze(1).to_broadcast([P, C, E_])

            dve.wait_ge(s["cst"], 8)
            dve.wait_ge(s["lgt"], 8)
            L = bank[6][:, 0:256].rearrange("p (c e) -> p c e", e=E_)
            step(dve.tensor_reduce(rs_[:, 0, :], L, AX.X, ALU.max))
            step(dve.tensor_tensor(ce(0), L, over_e(rs_[:, 0, :]), ALU.subtract))
            dve.wait_ge(s["rex"], 1)
            step(dve.tensor_reduce(rs_[:, 1, :], ce(1), AX.X, ALU.add))
            step(dve.reciprocal(rs_[:, 2, :], rs_[:, 1, :]))
            step(dve.tensor_tensor(ce(2), ce(1), over_e(rs_[:, 2, :]), ALU.mult))
            for k in range(TOP):
                src, hot = ce(2 + k), ce(4 + k)
                step(dve.tensor_reduce(prob[:, k, :], src, AX.X, ALU.max))
                step(dve.tensor_tensor(ce(6), src, over_e(prob[:, k, :]), ALU.is_equal))
                step(dve.tensor_tensor(ce(6), ce(6), over_c(w8[:]), ALU.mult))
                step(dve.tensor_reduce(rs_[:, 3, :], ce(6), AX.X, ALU.max))
                step(dve.tensor_tensor(hot, over_c(w8[:]), over_e(rs_[:, 3, :]), ALU.is_equal))
                if k + 1 < TOP:
                    step(dve.scalar_tensor_tensor(ce(3), hot, -2.0, src, ALU.mult, ALU.add))
            dve.tensor_tensor(M_[:], rt[:, 4, :], rt[:, 5, :], ALU.add).then_inc(s["wk"], 1)
            dve.wait_ge(s["rank"], 1)
            ec = [rt[:, k, :].rearrange("p (e c) -> p e c", c=C) for k in range(12)]
            step(dve.tensor_copy(ec[6], bank[7][:, 256:512].rearrange("p (c e) -> p e c", e=E_)))
            step(dve.tensor_tensor_scan(rt[:, 7, :], rt[:, 6, :], zero256[:], 0.0, ALU.add, ALU.add))
            step(dve.tensor_tensor(rt[:, 8, :], rt[:, 7, :], rt[:, 6, :], ALU.subtract))
            step(dve.tensor_tensor(re_[:, 0, :], ec[7][:, :, C - 1], ec[8][:, :, 0], ALU.subtract))
            step(dve.tensor_tensor(ec[9], re_[:, 0, :].unsqueeze(2).to_broadcast([P, E_, C]),
                                   thr[:].unsqueeze(1).to_broadcast([P, E_, C]), ALU.is_gt))
            step(dve.tensor_reduce(re_[:, 1, :], ec[9], AX.X, ALU.add))
            step(dve.tensor_tensor_scan(re_[:, 2, :], re_[:, 1, :], zero256[:, 0:E_], 0.0, ALU.add, ALU.add))
            step(dve.tensor_tensor(re_[:, 3, :], re_[:, 2, :], re_[:, 1, :], ALU.subtract))
            step(dve.scalar_tensor_tensor(re_[:, 4, :], re_[:, 3, :], float(P), ec[8][:, :, 0], ALU.mult, ALU.subtract))
            step(dve.tensor_tensor(ec[10], ec[8], re_[:, 4, :].unsqueeze(2).to_broadcast([P, E_, C]), ALU.add))
            step(dve.tensor_tensor(ce(11), bank[7][:, 0:256].rearrange("p (c e) -> p c e", e=E_),
                                   rt[:, 10, :].rearrange("p (e c) -> p c e", c=C), ALU.add))
            for k in range(TOP):
                step(dve.tensor_tensor(ce(6), ce(4 + k), ce(11), ALU.mult))
                step(dve.tensor_reduce(slot[:, k, :], ce(6), AX.X, ALU.add))
            step(dve.tensor_copy(sloti[:, 0, :], slot[:].rearrange("p k c -> p (k c)")))
            step(dve.tensor_scalar(sloti[:, 1, :], sloti[:, 0, :], 7, None, ALU.logical_shift_right))
            step(dve.tensor_scalar(sloti[:, 2, :], sloti[:, 0, :], P - 1, None, ALU.bitwise_and))
            step(dve.tensor_copy(slota[:], sloti[:, 1:3, :]))
            n2 = TOP * C
            dve.tensor_tensor(BH, slota[:, 1, :].unsqueeze(2).to_broadcast([P, n2, P]),
                              iota_w[:].unsqueeze(1).to_broadcast([P, n2, P]), ALU.is_equal).then_inc(s["vmm"], 1)
            dve.tensor_tensor(AW[:, :, 0, :], slota[:, 0, :].unsqueeze(2).to_broadcast([P, n2, TILES]),
                              iota_w[:, 0:TILES].unsqueeze(1).to_broadcast([P, n2, TILES]), ALU.is_equal)\
                .then_inc(s["vmm"], 1)
            dve.wait_ge(s["vmm"], 2)
            dve.tensor_scalar(AW[:, :, 1, :], AW[:, :, 0, :], iota_p[:, 0:1], None, ALU.mult).then_inc(s["vmm"], 1)
            dve.wait_ge(s["vmm"], 3)
            dve.tensor_tensor(AW[:, :, 0, :], AW[:, :, 0, :], cnum[:].unsqueeze(2).to_broadcast([P, n2, TILES]),
                              ALU.mult).then_inc(s["vmm"], 1)
            dve.tensor_tensor(te, re_[:, 2, :].unsqueeze(1).to_broadcast([P, ROWS_, E_]),
                              iota_w[:, 0:ROWS_].unsqueeze(2).to_broadcast([P, ROWS_, E_]), ALU.is_le)\
                .then_inc(s["te_set"], 1)
            dve.wait_ge(s["te_set"], 1)
            dve.tensor_reduce(tef[:], te, AX.X, ALU.add).then_inc(s["te_set"], 1)
            dve.wait_ge(s["te_set"], 2)
            dve.tensor_scalar(tile_e[:], tef[:], float(E_ - 1), None, ALU.min).then_inc(s["te_set"], 1)
            dve.wait_ge(s["ve"], 1)
            step(dve.tensor_copy(vt[:, 0, :], bank[0][:, TILES:2 * TILES]))
            step(dve.scalar_tensor_tensor(vt[:, 1, :], bank[0][:, 0:TILES], float(P), vt[:, 0, :], ALU.mult, ALU.add))
            step(dve.scalar_tensor_tensor(vt[:, 2, :], vt[:, 1, :], float(P), spare[:], ALU.is_lt, ALU.mult))
            step(dve.tensor_scalar(vt[:, 3, :], vt[:, 1, :], -float(P), None, ALU.add))
            dve.tensor_tensor(idx[:, 1, :], vt[:, 3, :], vt[:, 2, :], ALU.add).then_inc(s["te_set"], 1)
            step(dve.tensor_scalar(vt[:, 5, :], vt[:, 3, :], 0.0, None, ALU.max))
            step(dve.tensor_scalar(vt[:, 4, :], vt[:, 5, :], float(C * P), -float(C * P), ALU.is_ge, ALU.mult))
            dve.tensor_tensor(idx[:, 0, :], vt[:, 5, :], vt[:, 4, :], ALU.add).then_inc(s["te_set"], 1)
            dve.wait_ge(s["te_set"], 5)
            dve.wait_ge(s["w_in"], 64)

            def gather_index(r, n):
                if not isinstance(r, int) or BODY * r + n >= RING:
                    dve.wait_ge(g_in[n % RING], 16 * (BODY // RING * r + n // RING))
                dve.tensor_copy(gix[:, n % RING, :], idx[:, 0, bass.ds(BODY * r + n, 1)]).then_inc(s["fgi"], 1)

            def scatter_index(r, n):
                if not isinstance(r, int) or BODY * r + n >= RING:
                    dve.wait_ge(sct[n % RING], 16 * (BODY // RING * r + n // RING))
                dve.tensor_copy(six[:, n % RING, :], idx[:, 1, bass.ds(BODY * r + n, 1)]).then_inc(s["fsi"], 1)

            def x_copy(r, n):
                dve.wait_ge(s["ftx"], BODY * r + n + 1)
                past(dve, s["fm1"], r, n - 1)
                dve.tensor_copy(xgT[:, n % 2, :], bank[n % 2][:, 0:P]).then_inc(s["fxc"], 1)

            def add_b1(r, n):
                e = expert_of[n]
                dve.wait_ge(s["fm1"], BODY * r + n + 1)
                past(dve, s["fge"], r, n - 1)
                dve.tensor_tensor(hs[:, n % 2, :].rearrange("p (k t) -> p k t", k=K_),
                                  bank[2 + n % 2][:, :].rearrange("p (k t) -> p k t", k=K_),
                                  b1T[:, bass.ds(e * K_, K_)].unsqueeze(2).to_broadcast([P, K_, P]), ALU.add)\
                    .then_inc(s["fad"], 1)

            def add_b2(r, n):
                e = expert_of[n]
                dve.wait_ge(s["fm2"], BODY * r + n + 1)
                dve.tensor_tensor(ys[:, n % RING, :], bank[6 + n % 2][:, 0:P], b2s[:, bass.ds(e * P, P)], ALU.add)\
                    .then_inc(s["fy"], 1)

            tiles(dve, True, (gather_index, 6), (x_copy, 2), (add_b1, 1), (scatter_index, 0), (add_b2, 0))
            for n in range(4):
                dve.wait_ge(y_in[n], 32)
                for k, Y in enumerate((Y1, Y2)):
                    for c in range(8 * n, 8 * n + 8):
                        if k:
                            dve.wait_ge(s["fin"], 16 * n + c - 8 * n + 1)
                        dve.scalar_tensor_tensor(X[:, c, :], Y[:, c, :], prob[:, k, c:c + 1], X[:, c, :],
                                                 ALU.mult, ALU.add).then_inc(s["fin"], 1)


def kernel(**inputs):
    import numpy as np
    import concourse.bacc as _bacc
    from concourse.bass_utils import run_bass_kernel_spmd as _run

    c = {k[8:]: np.asarray(v) for k, v in inputs.items() if k.startswith("L0_conv_")}
    names = ["l1", "g1", "l2", "g2", "g5", "l3", "g3", "l4", "g4", "l5"]
    arrays = {
        "x": np.asarray(inputs["x"]), "z2": c["z2"], "z3": c["z3"],
        "conv_w": np.stack([c[n + "_w"] for n in names], axis=1),
        "conv_b": np.stack([c[n + "_b"] for n in names]),
        "ln_p": np.stack([np.stack([c[f"ln{i}_w"], c[f"ln{i}_b"]], axis=1) for i in (1, 2, 3, 5)], axis=1),
    }
    for n in ("W_g", "w1", "b1", "w2", "b2"):
        arrays[n] = np.asarray(inputs["L0_ffn_" + n])
    nc = _bacc.Bacc("TRN2", target_bir_lowering=False, num_devices=1)
    feeds, args = {}, []
    for name, a in arrays.items():
        a = np.ascontiguousarray(a)
        feeds[f"in_{name}"] = a
        args.append(nc.dram_tensor(f"in_{name}", a.shape, mybir.dt.from_np(a.dtype), kind="ExternalInput").ap())
    args.append(nc.dram_tensor("out", (1, C, P, P), F32, kind="ExternalOutput").ap())
    build(nc, *args)
    r = _run(nc, [feeds], core_ids=[0])
    return r.results[0]["out"]
```

```python
from contextlib import ExitStack

import concourse.bass as bass
from concourse import mybir

ALU = mybir.AluOpType
ACT = mybir.ActivationFunctionType
F32 = mybir.dt.float32
BF16 = mybir.dt.bfloat16
I32 = mybir.dt.int32
AX = mybir.AxisListType

P = 128
C = 32
Q = P // C
CH = P // Q
NCH = 4
SLOTS = 10
NA = 9
GROUPS = [(0, 5), (5, 7), (7, 9), (9, 10)]
E_ = 8
F = 512
K_ = F // P
TOP = 2
BODY = 8
TILES = TOP * C + E_ - 1
BODIES = -(-TILES // BODY)
ROWS_ = BODIES * BODY + 4
AHEAD = 7
RING = 8
EPS_C, EPS = 1e-6, 1e-5


def build(nc, x, z2, z3, conv_w, conv_b, ln_p, W_g, w1, b1, w2, b2, out):
    with ExitStack() as ctx:
        def sb(name, shape, dt=F32):
            return ctx.enter_context(nc.sbuf_tensor(name, shape, dt))

        def sem(name):
            return ctx.enter_context(nc.semaphore(name))

        bank = [ctx.enter_context(nc.psum_tensor(f"bank{i}", [P, 512], F32)) for i in range(8)]

        X = sb("X", [P, C, P])
        Z23 = sb("Z23", [P, 2, C, P])
        Z2, Z3 = Z23[:, 0], Z23[:, 1]
        ZA = sb("ZA", [P, C, P])
        ZB = sb("ZB", [P, C, P])
        ZD = sb("ZD", [P, P, C])
        p2T = sb("p2T", [P, C, P])
        p3T = sb("p3T", [P, C, P])
        z12, z13 = Z2, Z3
        R = sb("R", [P, SLOTS, Q, C])
        RS = sb("RS", [P, SLOTS, Q, C])
        lnp = sb("lnp", [P, 4, 2])
        lnb = sb("lnb", [P, 96])
        braw = sb("braw", [96, C])
        BD = sb("BD", [P, NA, Q, C])
        ldif = sb("ldif", [P, 3])
        blkd = sb("blkd", [P, 3, P])
        ZDf = ZD[:].rearrange("p a b -> p (a b)")
        bsum = ZDf[0:96, 0:P]
        bhi = ZDf[0:96, 2048:2048 + P // 2].bitcast(BF16)
        bmid = ZDf[0:96, 3072:3072 + P // 2].bitcast(BF16)
        BB = sb("BB", [96, P], BF16)
        pick3 = sb("pick3", [96, P], BF16)
        ident = sb("ident", [P, P])
        blk = sb("blk", [P, P])
        cen = sb("cen", [P, P])
        sq = sb("sq", [P, 2, 512])
        sd = sb("sd", [P, 2, 512])
        rn = sb("rn", [P, 2, 512])
        sg = sb("sg", [P, 2, 256])
        epsc = sb("epsc", [P, 1])
        onec = sb("onec", [P, 1])
        bn = sb("bn", [P, C, 6])
        st = sb("st", [P, 8, C])
        mu = sb("mu", [P, P])
        var = sb("var", [P, P])
        rsd = sb("rsd", [P, P])
        sig5 = ZA[:].rearrange("p a b -> p (a b)").rearrange("p (j c) -> p j c", c=C)
        Zt = ZB[:].rearrange("p a b -> p (a b)").rearrange("p (j c) -> p j c", c=C)
        T5 = p2T
        elu_b = p3T[:].rearrange("p a b -> p (a b)")[:, 0:2048].rearrange("p (k n f) -> p k n f", k=2, n=2)
        um, ue = elu_b[:, 0], elu_b[:, 1]
        PARTS = [(0, 8), (8, 16), (16, 24), (24, 28), (28, 32)]
        Z1_ACT = 24
        XL_ACT = 16
        PIECES = 4
        NZ = 16
        cen_bank = [0, 1, 4, 5, 6, 7]
        proj_bank = [6, 7, 4, 5]
        BIASES = [(5, 7, 6, 0), (7, 9, 6, 256), (9, 10, 7, 0), (4, 5, 7, 128), (0, 4, 5, 0)]
        NORM = [1, 2, 3, 0, 0]

        w1s = Z2.rearrange("p c j -> p (c j)")
        w2s = Z3.rearrange("p c j -> p (c j)")
        b1r = sb("b1r", [E_ * K_, P])
        b1T = sb("b1T", [P, E_ * K_])
        b2s = sb("b2s", [P, E_ * P])
        XL = ZB
        XT = p2T
        BH = p3T[:].rearrange("p a b -> p (a b)").bitcast(BF16).rearrange("p (r n) -> p r n", n=TOP * C)
        AW = sb("AW", [P, 2, TILES, TOP * C], BF16)
        count_r = ZDf.bitcast(BF16).rearrange("p (r n) -> p r n", n=TOP * C)
        wg = sb("wg", [P, E_])
        wg_cen = sb("wg_cen", [P, E_])
        mean_p = sb("mean_p", [P, P])
        ZAf = ZA[:].rearrange("p a b -> p (a b)")
        rt = ZAf[:, 0:12 * C * E_].rearrange("p (k n) -> p k n", k=12)
        te = ZAf[:, 12 * C * E_:12 * C * E_ + ROWS_ * E_].rearrange("p (t e) -> p t e", e=E_)
        rs_ = sb("rs_", [P, 10, C])
        re_ = sb("re_", [P, 8, E_])
        prob = sb("prob", [P, TOP, C])
        slot = sb("slot", [P, TOP, C])
        sloti = sb("sloti", [P, 3, TOP * C], I32)
        slota = sb("slota", [P, 2, TOP * C], BF16)
        M_ = sb("M_", [P, C * E_], BF16)
        lower = sb("lower", [P, P], BF16)
        ones = sb("ones", [P, P], BF16)
        iota_w = sb("iota_w", [P, P])
        iota_p = sb("iota_p", [P, 1])
        spare = sb("spare", [P, TILES])
        cnum = sb("cnum", [P, TOP * C], BF16)
        w8 = sb("w8", [P, E_])
        thr = sb("thr", [P, C])
        zero256 = sb("zero256", [P, C * E_])
        vt = sb("vt", [P, 6, TILES])
        idx = sb("idx", [P, TOP, TILES], I32)
        tef = sb("tef", [P, ROWS_])
        tile_e = sb("tile_e", [P, ROWS_], I32)
        gix = sb("gix", [P, RING, 1], I32)
        six = sb("six", [P, RING, 1], I32)
        XTf = XT[:].rearrange("p c i -> p (c i)")
        xg = XTf[:, 0:1024].rearrange("p (n h) -> p n h", n=RING)
        xgT = sb("xgT", [P, 2, P])
        hs = XTf[:, 1024:2048].rearrange("p (n f) -> p n f", n=2)
        hg = XTf[:, 2048:3072].rearrange("p (n f) -> p n f", n=2)
        w1t = XTf[:, 3072:4096].rearrange("p (n f) -> p n f", n=2)
        in_tile = XTf.bitcast(BF16)[:, 0:TILES * TOP * C].rearrange("p (t n) -> p t n", t=TILES)
        ys = sb("ys", [P, RING, P])
        Y1, Y2 = p2T, p3T
        xrows = nc.dram_tensor("xrows", (C * P, P), F32)
        yrows = nc.dram_tensor("yrows", ((TOP * C + TILES) * P, P), F32)
        g_in = [sem(f"g_in{i}") for i in range(RING)]
        y_in = [sem(f"y_in{i}") for i in range(10)]
        sct = [sem(f"sct{i}") for i in range(RING)]

        s = {n: sem(n) for n in (
            "w_in xr_out tbn tst trs wg_in wg_sum wg_set xln xla xl_bias txl txlc lgt rt_ rex wk rank vmm aw_set ve idx_set te_set cst b1_in b1_turned b1_set count_set "
            "ftx fxc fw1 fm1 fad fge fm2 fy fsi fgi pool_go y_scaled y_sum fin").split()}
        s |= {n: sem(n) for n in (
            "ones_set r_zero diag_in lnp_in braw_in bd_in x_in z2a_in z2b_in z3_in "
            "consts lnb_set bd_set bias_mm bsum_set b_step bb_set rs_set mh_set "
            "cenz sqz varz lnz rnz zn z_one z_plus "
            "pr2 sg2 gate2 pr3 sg3 gate3 "
            "xbn xst xrs z1 z1a z1_bias amu acen asq avar ars anorm "
            "t1 t1c t1d pra sga gata g5mm g5s tz tzc tzd ein einc "
            "t5 t5c t5d cen5 sq5 var5 ln5 rn5 norm5 pr5 u5 um5 ue5 y5 x2 out_done").split()}

        block = ctx.enter_context(nc.Block())
        x_v = x.rearrange("a c i j -> i (a c) j")
        out_v = out.rearrange("a c i j -> i (a c) j")

        def rsqrt(act, out, v, ready, count, done, before):
            act.wait_ge(s[ready], count)
            act.activation(out, v, ACT.Ln).then_inc(s[done], 1)
            act.wait_ge(s[done], before + 1)
            act.activation(out, out, ACT.Exp, scale=-0.5).then_inc(s[done], 1)

        def z1(eng, a, b, signal):
            eng.wait_ge(s["xrs"], 2)
            for c in range(a, b):
                eng.tensor_scalar(ZA[:, c, :], X[:, c, :], st[:, 2, c:c + 1], st[:, 6, c:c + 1],
                                  ALU.subtract, ALU.mult).then_inc(s[signal], 1)

        T5_DVE = (1, 4)

        def t5_copied(eng, n):
            by_dve = sum(t <= n for t in T5_DVE)
            if n in T5_DVE:
                eng.wait_ge(s["t5d"], by_dve)
            else:
                eng.wait_ge(s["t5c"], n + 1 - by_dve)

        def elu_exp(act, n):
            act.wait_ge(s["um5"], n + 1)
            if n >= 2:
                act.wait_ge(s["y5"], n - 1)
            act.activation(ue[:, n % 2, :], um[:, n % 2, :], ACT.Exp).then_inc(s["ue5"], 1)

        def elu_add(dve, n):
            U = sig5[:, 16 * n:16 * n + 16, :].rearrange("p j c -> p (j c)")
            dve.wait_ge(s["ue5"], n + 1)
            dve.scalar_tensor_tensor(U, ue[:, n % 2, :], -1.0, U, ALU.add, ALU.max).then_inc(s["y5"], 1)

        def x_add(pool, n):
            pool.wait_ge(s["y5"], n + 1)
            xs = X[:, :, 16 * n:16 * n + 16].rearrange("p c j -> p j c")
            pool.tensor_tensor(xs, xs, sig5[:, 16 * n:16 * n + 16, :], ALU.add).then_inc(s["x2"], 1)

        def row_stats(dve, eps, tag, base):
            me, mo, ve, vo = bn[:, :, 1], bn[:, :, 4], bn[:, :, 2], bn[:, :, 5]
            dve.tensor_tensor(st[:, 0, :], me, mo, ALU.add).then_inc(s[tag], 1)
            dve.tensor_tensor(st[:, 1, :], me, mo, ALU.subtract).then_inc(s[tag], 1)
            dve.tensor_tensor(st[:, 3, :], ve, vo, ALU.add).then_inc(s[tag], 1)
            dve.wait_ge(s[tag], base + 3)
            dve.tensor_scalar(st[:, 2, :], st[:, 0, :], 0.5, None, ALU.mult)
            dve.scalar_tensor_tensor(st[:, 4, :], st[:, 1, :], 0.25, st[:, 1, :], ALU.mult, ALU.mult)\
                .then_inc(s[tag], 1)
            dve.tensor_scalar(st[:, 7, :], st[:, 3, :], 1.0 / P, eps, ALU.mult, ALU.add).then_inc(s[tag], 1)
            dve.wait_ge(s[tag], base + 5)
            dve.tensor_tensor(st[:, 5, :], st[:, 7, :], st[:, 4, :], ALU.add).then_inc(s[tag], 1)

        def past(eng, signal, r, n):
            if not isinstance(r, int) or BODY * r + n > 0:
                eng.wait_ge(signal, BODY * r + n)

        expert_of = {}

        def load_experts(eng, r, quad):
            _, vals = nc.values_load_multi_w_load_instructions(
                tile_e[0:1, bass.ds(BODY * r + 4 * quad, 4)], engines=(eng.engine,), min_val=0, max_val=E_ - 1,
                skip_runtime_bounds_check_because="the table's entries are a count of 0 to 8, cut at 7")
            for n, v in enumerate(vals):
                expert_of[4 * quad + n] = v

        def tiles(eng, experts, *stages):
            def body(r, first):
                for n in range(first, BODY if not isinstance(r, int) else min(BODY, TILES - BODY * r)):
                    if experts and n == 0:
                        load_experts(eng, r, 0)
                    if experts and n >= 0 and n % 4 == 1:
                        load_experts(eng, r, n // 4 + 1)
                    for stage, ahead in stages:
                        if not isinstance(r, int) or 0 <= BODY * r + n + ahead < TILES:
                            stage(r, n + ahead)
            if experts:
                load_experts(eng, 0, 0)
            body(0, -AHEAD)
            with eng.Fori(1, BODIES - 1) as r:
                body(r, 0)
            body(BODIES - 1, 0)

        def busy_work(pe, n, slots=4):
            for _ in range(n):
                pe.matmul(bank[3][:, 0:slots * P], blk[:], RS[:, 0:slots].rearrange("p s q c -> p (s q c)"),
                          start=True, stop=True)

        def logits(pe, n):
            pe.wait_ge(s["txlc"], n + 1)
            for c in range(4 * n, 4 * n + 4):
                mm = pe.matmul(bank[6][:, c * E_:(c + 1) * E_], XT[:, c, :], wg_cen[:], start=True, stop=True)
            mm.then_inc(s["lgt"], 1)

        @block.sync
        def _(sp):
            for h in range(0, C, C // 2):
                for q in range(Q):
                    sp.dma_start(Z2[q * C:(q + 1) * C, h:h + C // 2, :], z2[0, :, q * C + h:q * C + h + C // 2, :])\
                        .then_inc(s["z2b_in" if h else "z2a_in"], 16)
            sp.wait_ge(s["r_zero"], 2)
            for q in range(Q):
                sp.dma_start(R[q * C:(q + 1) * C, :, q, :], conv_w).then_inc(s["diag_in"], 16)
            for q in range(Q):
                sp.dma_start(lnp[q * C:(q + 1) * C, :, :], ln_p).then_inc(s["lnp_in"], 16)
            sp.dma_start(braw[:, :], conv_b[NA, :].partition_broadcast(96)).then_inc(s["braw_in"], 16)
            sp.dma_start(X[:, :, :], x_v).then_inc(s["x_in"], 16)
            for q in range(Q):
                sp.dma_start(Z3[q * C:(q + 1) * C, :, :], z3[0, :, q * C:(q + 1) * C, :]).then_inc(s["z3_in"], 16)
            for q in range(Q):
                sp.dma_start(BD[q * C:(q + 1) * C, :, q, :], conv_b[0:NA, :].partition_broadcast(C))\
                    .then_inc(s["bd_in"], 16)
            sp.dma_start(b1r[:], b1.rearrange("e (k f) -> (e k) f", k=K_)).then_inc(s["b1_in"], 16)
            sp.dma_start(wg[:], W_g).then_inc(s["wg_in"], 16)
            sp.dma_start(b2s[:], b2.rearrange("e h -> (e h)").partition_broadcast(P)).then_inc(s["w_in"], 16)
            sp.wait_ge(s["ein"], 8)
            sp.dma_start(w1s.rearrange("p (e f) -> p e f", e=E_), w1.rearrange("e h f -> h e f")).then_inc(s["w_in"], 16)
            sp.dma_start(w2s.rearrange("p (e k h) -> p e k h", e=E_, h=P), w2.rearrange("e (k p) h -> p e k h", p=P))\
                .then_inc(s["w_in"], 16)
            xr = xrows.ap().rearrange("(c i) j -> i c j", i=P)
            for n in range(4):
                if 8 * n < XL_ACT:
                    sp.wait_ge(s["xln"], 8 * n + 8)
                else:
                    sp.wait_ge(s["xla"], 8 * n + 8 - XL_ACT)
                sp.dma_start(xr[:, 8 * n:8 * n + 8, :], XL[:, 8 * n:8 * n + 8, :]).then_inc(s["xr_out"], 16)
            for u in range(RING):
                sp.wait_ge(sct[u], 16 * -(-(TILES - u) // RING))
            yr = yrows.ap()[0:TOP * C * P, :].rearrange("(k c i) j -> k i c j", k=TOP, i=P)
            for n, (a, b) in enumerate(PARTS):
                for k, Y in reversed(list(enumerate((Y1, Y2)))):
                    sp.dma_start(Y[:, a:b, :], yr[k][:, a:b, :]).then_inc(y_in[2 * n + k], 16)
            for n, (a, b) in enumerate(PARTS):
                sp.wait_ge(s["fin"], n + 1)
                sp.dma_start(out_v[:, a:b, :], X[:, a:b, :]).then_inc(s["out_done"], 16)
            sp.wait_ge(s["out_done"], 16 * len(PARTS))

        @block.gpsimd
        def _(pool):
            pool.memset(ident[:], 0.0).then_inc(s["ones_set"], 1)
            pool.wait_ge(s["ones_set"], 1)
            pool.affine_select(out=ident[:], in_=ident[:], compare_op=ALU.not_equal, fill=1.0, base=0,
                               pattern=[[-1, P]], channel_multiplier=1).then_inc(s["ones_set"], 1)
            pool.memset(onec[:], 1.0).then_inc(s["z_one"], 1)
            pool.memset(lower[:], 1.0).then_inc(s["cst"], 1)
            pool.wait_ge(s["cst"], 1)
            pool.affine_select(out=lower[:], in_=lower[:], compare_op=ALU.is_gt, fill=0.0, base=0,
                               pattern=[[1, P]], channel_multiplier=-1).then_inc(s["cst"], 1)
            imp = dict(allow_small_or_imprecise_dtypes=True)
            pool.iota(iota_w[:], pattern=[[1, P]], base=0, channel_multiplier=0, **imp).then_inc(s["cst"], 1)
            pool.iota(iota_p[:], pattern=[[0, 1]], base=0, channel_multiplier=1, **imp).then_inc(s["cst"], 1)
            pool.iota(spare[:], pattern=[[P, TILES]], base=(TOP * C + 1) * P, channel_multiplier=1, **imp)\
                .then_inc(s["cst"], 1)
            pool.iota(cnum[:], pattern=[[1, TOP * C]], base=1, channel_multiplier=0, **imp).then_inc(s["cst"], 1)
            pool.iota(w8[:], pattern=[[-1, E_]], base=E_, channel_multiplier=0, **imp).then_inc(s["cst"], 1)
            pool.iota(thr[:], pattern=[[P, C]], base=0, channel_multiplier=0, **imp).then_inc(s["cst"], 1)
            pool.wait_ge(s["bsum_set"], 1)
            pool.tensor_copy(bhi[:], bsum).then_inc(s["b_step"], 1)
            pool.wait_ge(s["b_step"], 1)
            pool.tensor_tensor(bsum, bsum, bhi[:], ALU.subtract).then_inc(s["b_step"], 1)
            pool.wait_ge(s["b_step"], 2)
            pool.tensor_copy(bmid[:], bsum).then_inc(s["b_step"], 1)
            pool.wait_ge(s["b_step"], 3)
            pool.tensor_tensor(bsum, bsum, bmid[:], ALU.subtract).then_inc(s["b_step"], 1)
            pool.wait_ge(s["z_one"], 1)
            for g in range(NZ):
                pool.wait_ge(s["zn"], g + 1)
                zs = Z23[:, g // 8, 4 * (g % 8):4 * (g % 8) + 4, :].rearrange("p i j -> p (i j)")
                pool.tensor_tensor(zs, zs, onec[:, 0:1].to_broadcast([P, 512]), ALU.add).then_inc(s["z_plus"], 1)
            for k in range(NCH):
                d = slice(k * CH, (k + 1) * CH)
                pool.wait_ge(s["amu"], 2 * k + 2)
                pool.tensor_tensor(ZA[:, :, d], ZA[:, :, d], mu[:, d].unsqueeze(1).to_broadcast([P, C, CH]),
                                   ALU.subtract).then_inc(s["acen"], 1)
            pool.wait_ge(s["acen"], NCH)
            pool.wait_ge(s["ars"], 2)
            pool.wait_ge(s["bb_set"], 3)
            for k in range(NCH):
                d = slice(k * CH, (k + 1) * CH)
                pool.tensor_tensor(ZD[:, d, :], ZA[:, :, d].rearrange("p c j -> p j c"),
                                   rsd[:, d].unsqueeze(2).to_broadcast([P, CH, C]), ALU.mult).then_inc(s["anorm"], 1)
            for n in range(7):
                x_add(pool, n)
            pool.wait_ge(s["ein"], 8)
            pool.iota(count_r, pattern=[[1, P], [0, TOP * C]], base=0, channel_multiplier=0, **imp)\
                .then_inc(s["count_set"], 1)

            def gather(r, n):
                pool.wait_ge(s["fgi"], BODY * r + n + 1)
                past(pool, s["ftx"], r, n - RING + 1)
                pool.sem_inc(s["pool_go"], 1)
                pool.indirect_dma_start(out=xg[:, n % RING, :], out_offset=None, in_=xrows.ap(),
                                        in_offset=bass.IndirectOffsetOnAxis(ap=gix[:, n % RING, :], axis=0))\
                    .then_inc(g_in[n % RING], 16)

            def scatter(r, n):
                pool.wait_ge(s["fsi"], BODY * r + n + 1)
                pool.wait_ge(s["fy"], BODY * r + n + 1)
                pool.sem_inc(s["pool_go"], 1)
                pool.indirect_dma_start(out=yrows.ap(), in_=ys[:, n % RING, :], in_offset=None,
                                        out_offset=bass.IndirectOffsetOnAxis(ap=six[:, n % RING, :], axis=0))\
                    .then_inc(sct[n % RING], 16)

            pool.wait_ge(s["xr_out"], 64)
            tiles(pool, False, (gather, AHEAD), (scatter, 0))

        @block.tensor
        def _(pe):
            def centre(g):
                pe.wait_ge(s["z2a_in" if g < 4 else "z2b_in" if g < 8 else "z3_in"], 64)
                if g == 3:
                    pe.wait_ge(s["bsum_set"], 1)
                    pe.wait_ge(s["rs_set"], 5)
                if g >= 6:
                    pe.wait_ge(s["zn"], g - 5)
                pe.matmul(bank[cen_bank[g % 6]][:, :], cen[:], Z23[:, g // 8, 4 * (g % 8):4 * (g % 8) + 4, :]
                          .rearrange("p i j -> p (i j)"), start=True, stop=True).then_inc(s["cenz"], 1)

            pe.wait_ge(s["consts"], 1)
            centre(0)
            centre(1)
            centre(2)
            pe.wait_ge(s["diag_in"], 64)
            pe.wait_ge(s["lnb_set"], 4)
            for n, (a, b, bk, col) in enumerate(BIASES):
                rows, lhsT = (96, lnb[:]) if n == 2 else (P, blkd[:, NORM[n], :])
                pe.matmul(bank[bk][0:rows, col:col + (b - a) * P], lhsT,
                          R[:, a:b].rearrange("p s q c -> p (s q c)"), start=True, stop=True).then_inc(s["bias_mm"], 1)
            for g in range(NZ):
                if 0 < g < NZ - 2:
                    centre(g + 2)
                pe.wait_ge(s["sqz"], g + 1)
                if g >= 2:
                    pe.wait_ge(s["lnz"], g - 1)
                pe.matmul(bank[2 + g % 2][:, :], blk[:], sq[:, g % 2, :], start=True, stop=True)\
                    .then_inc(s["varz"], 1)

            def proj(z, tag, a, m, before):
                if before + m >= 4:
                    pe.wait_ge(s["gate2"], min(16, before + m - 3))
                    if before + m - 3 > 16:
                        pe.wait_ge(s["gate3"], before + m - 3 - 16)
                if before + m < 4:
                    pe.wait_ge(s["zn"], (11, 12, 15, 16)[m])
                pe.wait_ge(s["z_plus"], before // 2 + m // 2 + 1)
                pe.wait_ge(s["rs_set"], 6)
                o = bank[proj_bank[m % 4]]
                for h in range(2):
                    mm = pe.matmul(o[:, 256 * h:256 * h + 256], z[:, 2 * m + h, :],
                                   RS[:, a:a + 2].rearrange("p s q c -> p (s q c)"), start=True, stop=True)
                mm.then_inc(s["pr" + tag], 1)

            for m in range(16):
                proj(Z2, "2", 5, m, 0)
            for m in range(16):
                proj(Z3, "3", 7, m, 16)

            def t1(k):
                pe.wait_ge(s["anorm"], k + 1)
                for h in range(2):
                    n = 2 * k + h
                    if n >= 2:
                        pe.wait_ge(s["t1c" if n % 2 == 0 else "t1d"], n // 2)
                    for v in range(4):
                        j0 = (4 * n + v) * 4
                        mm = pe.transpose(bank[n % 2][:, v * P:(v + 1) * P],
                                          ZD[:, j0:j0 + 4, :].rearrange("p j c -> p (j c)"), ident[:])
                    mm.then_inc(s["t1"], 1)
            for k in range(NCH):
                t1(k)
            pe.wait_ge(s["b1_in"], 16)
            pe.wait_ge(s["t1c"], 4)
            pe.transpose(bank[0][:, 0:E_ * K_], b1r[:], ident[0:E_ * K_, 0:E_ * K_]).then_inc(s["b1_turned"], 1)
            pe.wait_ge(s["wg_in"], 16)
            pe.wait_ge(s["t1d"], 4)
            pe.matmul(bank[1][:, 0:E_], mean_p[:], wg[:], start=True, stop=True).then_inc(s["wg_sum"], 1)
            for n in range(C):
                pe.wait_ge(s["t1c" if n // 4 % 2 == 0 else "t1d"], n // 8 + 1)
                if n >= 4:
                    pe.wait_ge(s["gata"], n - 3)
                else:
                    pe.wait_ge(s["gate3"], 13 + n)
                pe.wait_ge(s["rs_set"], 6)
                pe.matmul(bank[proj_bank[n % 4]][:, :], ZB[:, n, :], RS[:, 0:4].rearrange("p s q c -> p (s q c)"),
                          start=True, stop=True).then_inc(s["pra"], 1)
                g = n // 4
                if n % 4 == 0:
                    if g >= 2:
                        pe.wait_ge(s["g5s"], g - 1)
                mm = pe.matmul(bank[2 + g % 2][:, (n % 4) * P:(n % 4 + 1) * P], ZB[:, n, :],
                               RS[:, 4].rearrange("p q c -> p (q c)"), start=True, stop=True)
                if n % 4 == 3:
                    mm.then_inc(s["g5mm"], 1)
            pe.wait_ge(s["gata"], C)
            for n in range(-2, 8):
                if n < 6:
                    t = n + 2
                    if t >= 2:
                        pe.wait_ge(s["tzc" if t % 2 == 0 else "tzd"], t // 2)
                    else:
                        pe.wait_ge(s["b1_set"], 1)
                        pe.wait_ge(s["wg_set"], 1)
                    for v in range(4):
                        mm = pe.transpose(bank[t % 2][:, v * P:(v + 1) * P], z13[:, 4 * t + v, :], ident[:])
                    mm.then_inc(s["tz"], 1)
                if n >= 0:
                    pe.wait_ge(s["tzc" if n % 2 == 0 else "tzd"], n // 2 + 1)
                    if n >= 4:
                        pe.wait_ge(s["einc"], n - 3)
                    for v in range(4):
                        c = 4 * n + v
                        o = bank[4 + n % 4][:, v * P:(v + 1) * P]
                        pe.matmul(o, p2T[:, c, :], z12[:, c, :], start=True, stop=False)
                        mm = pe.matmul(o, ZDf[:, c * P:(c + 1) * P], p3T[:, c, :], start=False, stop=True)
                    mm.then_inc(s["ein"], 1)
            def t5(n):
                if n:
                    t5_copied(pe, n - 1)
                else:
                    pe.wait_ge(s["einc"], 8)
                for v in range(4):
                    mm = pe.transpose(bank[0][:, v * P:(v + 1) * P],
                                      Zt[:, 16 * n + 4 * v:16 * n + 4 * v + 4, :].rearrange("p j c -> p (j c)"),
                                      ident[:])
                mm.then_inc(s["t5"], 1)

            def centre5(n):
                t5_copied(pe, n)
                if n >= 3:
                    pe.wait_ge(s["norm5"], n - 2)
                pe.matmul(bank[1 + n % 3][:, :], cen[:], T5[:, 4 * n:4 * n + 4, :].rearrange("p a b -> p (a b)"),
                          start=True, stop=True).then_inc(s["cen5"], 1)

            def var5(n):
                pe.wait_ge(s["sq5"], n + 1)
                if n >= 2:
                    pe.wait_ge(s["ln5"], n - 1)
                pe.matmul(bank[4 + n % 2][:, :], blk[:], sq[:, n % 2, :], start=True, stop=True).then_inc(s["var5"], 1)

            def proj5(n):
                pe.wait_ge(s["norm5"], n + 1)
                if n >= 2:
                    pe.wait_ge(s["u5"], n - 1)
                o = bank[6 + n % 2]
                pe.wait_ge(s["bb_set"], 3)
                pe.matmul(o[:, :], pick3[:], BB[:, :].unsqueeze(1).to_broadcast([96, 4, P]),
                          start=True, stop=False)
                for v in range(4):
                    mm = pe.matmul(o[:, v * P:(v + 1) * P], T5[:, 4 * n + v, :], RS[:, 9].rearrange("p q c -> p (q c)"),
                                   start=False, stop=(v == 3))
                mm.then_inc(s["pr5"], 1)
            for n in range(-2, 9):
                for stage, ahead in ((t5, 2), (centre5, 1), (var5, 0), (proj5, -1)):
                    if 0 <= n + ahead < 8:
                        stage(n + ahead)
            busy_work(pe, 3)
            for n in range(8):
                pe.wait_ge(s["x2"], 8)
                if n >= 2:
                    pe.wait_ge(s["txlc"], n - 1)
                for v in range(4):
                    mm = pe.transpose(bank[4 + n % 2][:, v * P:(v + 1) * P], X[:, 4 * n + v, :], ident[:])
                mm.then_inc(s["txl"], 1)
                busy_work(pe, 1, 1)
                if n > 0:
                    logits(pe, n - 1)
            logits(pe, 7)
            pe.wait_ge(s["wk"], 1)
            pe.wait_ge(s["mh_set"], 14)
            pe.matmul(bank[7][:, 0:256], lower[:], M_[:], start=True, stop=True)
            pe.matmul(bank[7][:, 256:512], ones[:], M_[:], start=True, stop=True).then_inc(s["rank"], 1)
            for n in range(TOP * C):
                piece = TOP * C // PIECES
                if n % piece == 0:
                    pe.wait_ge(s["aw_set"], n // piece + 1)
                    pe.wait_ge(s["vmm"], 3 * (n // piece + 1))
                mm = pe.matmul(bank[0][:, 0:2 * TILES], BH[:, :, n], AW[:, :, :, n].rearrange("p a t -> p (a t)"),
                               start=(n == 0), stop=(n == TOP * C - 1))
            mm.then_inc(s["ve"], 1)
            pe.wait_ge(s["te_set"], 3)

            def x_turn(r, n):
                pe.wait_ge(g_in[n % RING], 16 * (BODY // RING * r + n // RING + 1))
                past(pe, s["fxc"], r, n - 1)
                pe.transpose(bank[n % 2][:, 0:P], xg[:, n % RING, :], ident[:]).then_inc(s["ftx"], 1)

            def up(r, n):
                pe.wait_ge(s["fxc"], BODY * r + n + 1)
                past(pe, s["fad"], r, n - 1)
                pe.wait_ge(s["fw1"], BODY * r + n + 1)
                for k in range(K_):
                    mm = pe.matmul(bank[2 + n % 2][:, k * P:(k + 1) * P], w1t[:, n % 2, k * P:(k + 1) * P],
                                   xgT[:, n % 2, :], start=True, stop=True)
                mm.then_inc(s["fm1"], 1)

            def down(r, n):
                e = expert_of[n]
                pe.wait_ge(s["fge"], BODY * r + n + 1)
                past(pe, s["fy"], r, n - 1)
                for k in range(K_):
                    mm = pe.matmul(bank[6 + n % 2][:, 0:P], hg[:, n % 2, k * P:(k + 1) * P],
                                   w2s[:, bass.ds(e * F + k * P, P)], start=(k == 0), stop=(k == K_ - 1))
                mm.then_inc(s["fm2"], 1)

            tiles(pe, True, (x_turn, 2), (up, 1), (down, 0))

        @block.scalar
        def _(act):
            act.preload_act_table_set("natural_log_exp_and_others")
            act.wait_ge(s["mh_set"], 7)

            def square(g):
                act.wait_ge(s["cenz"], g + 1)
                if g >= 2:
                    act.wait_ge(s["varz"], g - 1)
                act.activation(sq[:, g % 2, :], bank[cen_bank[g % 6]][:, :], ACT.Square).then_inc(s["sqz"], 1)
            square(0)
            for g in range(NZ):
                if g + 1 < NZ:
                    square(g + 1)
                act.wait_ge(s["varz"], g + 1)
                if g >= 2:
                    act.wait_ge(s["zn"], g - 1)
                act.activation(sd[:, g % 2, :], bank[2 + g % 2][:, :], ACT.Ln, bias=epsc[:, 0:1])\
                    .then_inc(s["lnz"], 1)
                act.wait_ge(s["lnz"], g + 1)
                act.activation(rn[:, g % 2, :], sd[:, g % 2, :], ACT.Exp, scale=-0.5).then_inc(s["rnz"], 1)
                if g == 10:
                    rsqrt(act, st[:, 6, :], st[:, 5, :], "xst", 6, "xrs", 0)

            def sigma(tag, m, before):
                act.wait_ge(s["pr" + tag], m + 1)
                if m >= 2:
                    act.wait_ge(s["gate" + tag], m - 1)
                elif before:
                    act.wait_ge(s["gate2"], 15 + m)
                act.activation(sg[:, m % 2, :].rearrange("p (h n) -> p h n", h=2),
                               bank[proj_bank[m % 4]][:].rearrange("p (h t n) -> p h t n", h=2, t=2)[:, :, 1, :],
                               ACT.Sigmoid).then_inc(s["sg" + tag], 1)

            def t1_copy(n):
                act.wait_ge(s["t1"], n + 1)
                act.activation(ZB[:, 4 * n:4 * n + 4, :].rearrange("p a b -> p (a b)"), bank[n % 2][:, :], ACT.Copy,
                               bias=1.0)\
                    .then_inc(s["t1c"], 1)
            for m in range(16):
                sigma("2", m, 0)
                if m < (C - Z1_ACT) // 2:
                    act.wait_ge(s["z1_bias"], 1)
                    for c in range(Z1_ACT + 2 * m, Z1_ACT + 2 * m + 2):
                        act.activation(ZA[:, c, :], X[:, c, :], ACT.Identity, scale=st[:, 6, c:c + 1],
                                       bias=st[:, 4, c:c + 1]).then_inc(s["z1a"], 1)
                if m in (6, 8, 10, 12):
                    k = m // 2 - 3
                    act.wait_ge(s["acen"], k + 1)
                    act.activation(ZB[:].rearrange("p a b -> p (a b)")[:, k * CH * C:(k + 1) * CH * C],
                                   ZA[:, :, k * CH:(k + 1) * CH].rearrange("p c j -> p j c"), ACT.Square)\
                        .then_inc(s["asq"], 1)
            for m in range(16):
                sigma("3", m, 16)
                if m == 0:
                    act.preload_act_table_set("natural_log_exp_and_others")
                    rsqrt(act, rsd[:], var[:], "avar", 8, "ars", 0)
            for n in range(0, 8, 2):
                t1_copy(n)
            act.wait_ge(s["b1_turned"], 1)
            act.activation(b1T[:], bank[0][:, 0:E_ * K_], ACT.Copy).then_inc(s["b1_set"], 1)
            for n in range(C):
                act.wait_ge(s["pra"], n + 1)
                if n >= 2:
                    act.wait_ge(s["gata"], n - 1)
                else:
                    act.wait_ge(s["gate3"], 15 + n)
                act.activation(sg[:, n % 2, :].rearrange("p (h n) -> p h n", h=2),
                               bank[proj_bank[n % 4]][:].rearrange("p (h t n) -> p h t n", h=2, t=2)[:, :, 1, :],
                               ACT.Sigmoid).then_inc(s["sga"], 1)
                if n % 4 == 3:
                    g = n // 4
                    act.wait_ge(s["g5mm"], g + 1)
                    act.activation(sig5[:, 16 * g:16 * g + 16, :].rearrange("p j c -> p (j c)"),
                                   bank[2 + g % 2][:, :], ACT.Sigmoid).then_inc(s["g5s"], 1)

            def tz_copy(n):
                act.wait_ge(s["tz"], n + 1)
                act.activation(ZDf[:, 512 * n:512 * n + 512], bank[n % 2][:, :], ACT.Copy).then_inc(s["tzc"], 1)

            def z_copy(n):
                act.wait_ge(s["ein"], n + 1)
                act.activation(Zt[:, :, 4 * n:4 * n + 4].rearrange("p j c -> p c j"),
                               bank[4 + n % 4][:, :].rearrange("p (c j) -> p c j", c=4), ACT.Copy).then_inc(s["einc"], 1)

            for n in range(-2, 8):
                if n < 6 and n % 2 == 0:
                    tz_copy(n + 2)
                if n >= 0:
                    z_copy(n)
            def t5_copy(n):
                if n in T5_DVE:
                    return
                act.wait_ge(s["t5"], n + 1)
                act.activation(T5[:, 4 * n:4 * n + 4, :].rearrange("p a b -> p (a b)"), bank[0][:, :],
                               ACT.Copy).then_inc(s["t5c"], 1)

            def square5(n):
                act.wait_ge(s["cen5"], n + 1)
                if n >= 2:
                    act.wait_ge(s["var5"], n - 1)
                act.activation(sq[:, n % 2, :], bank[1 + n % 3][:, :], ACT.Square).then_inc(s["sq5"], 1)

            def rsqrt5(n):
                act.wait_ge(s["var5"], n + 1)
                if n >= 2:
                    act.wait_ge(s["norm5"], n - 1)
                act.activation(sd[:, n % 2, :], bank[4 + n % 2][:, :], ACT.Ln, bias=epsc[:, 0:1]).then_inc(s["ln5"], 1)
                act.wait_ge(s["ln5"], n + 1)
                act.activation(rn[:, n % 2, :], sd[:, n % 2, :], ACT.Exp, scale=-0.5).then_inc(s["rn5"], 1)
            act.preload_act_table_set("natural_log_exp_and_others")
            for n in range(-2, 10):
                for stage, ahead in ((t5_copy, 2), (square5, 1), (rsqrt5, 0)):
                    if 0 <= n + ahead < 8:
                        stage(n + ahead)
                if 0 <= n - 2 < 8:
                    elu_exp(act, n - 2)
            for n in range(8):
                if n == 4:
                    rsqrt(act, st[:, 6, :], st[:, 5, :], "tst", 6, "trs", 0)
                act.wait_ge(s["txl"], n + 1)
                act.activation(XT[:, 4 * n:4 * n + 4, :].rearrange("p a b -> p (a b)"), bank[4 + n % 2][:, :],
                               ACT.Copy).then_inc(s["txlc"], 1)
            act.wait_ge(s["rt_"], 3)
            act.activation(rt[:, 1, :], rt[:, 0, :], ACT.Exp).then_inc(s["rex"], 1)
            act.wait_ge(s["xl_bias"], 1)
            for c in range(XL_ACT, C):
                act.activation(XL[:, c, :], X[:, c, :], ACT.Identity, scale=st[:, 6, c:c + 1],
                               bias=st[:, 4, c:c + 1]).then_inc(s["xla"], 1)
            for g in range(PIECES):
                n = slice(g * TOP * C // PIECES, (g + 1) * TOP * C // PIECES)
                act.wait_ge(s["vmm"], 3 * g + 1)
                act.activation(AW[:, 1, :, n], in_tile[:, :, n], ACT.Copy, scale=iota_p[:, 0:1])\
                    .then_inc(s["aw_set"], 1)
            act.preload_act_table_set("gelu_and_others")
            act.wait_ge(s["te_set"], 3)
            act.wait_ge(s["w_in"], 48)

            def gelu(r, n):
                act.wait_ge(s["fad"], BODY * r + n + 1)
                past(act, s["fm2"], r, n - 1)
                act.activation(hg[:, n % 2, :], hs[:, n % 2, :], ACT.Gelu).then_inc(s["fge"], 1)

            def w1_copy(r, n):
                e = expert_of[n]
                past(act, s["fm1"], r, n - 1)
                act.activation(w1t[:, n % 2, :], w1s[:, bass.ds(e * F, F)], ACT.Copy).then_inc(s["fw1"], 1)

            tiles(act, True, (w1_copy, 2), (gelu, 1))
            for n, (a, b) in enumerate(PARTS):
                act.wait_ge(y_in[2 * n + 1], 16)
                for c in range(a, b):
                    act.activation(Y2[:, c, :], Y2[:, c, :], ACT.Copy, scale=prob[:, 1, c:c + 1])\
                        .then_inc(s["y_scaled"], 1)

        @block.vector
        def _(dve):
            dve.memset(R[:], 0.0).then_inc(s["r_zero"], 1)
            dve.memset(BD[:], 0.0).then_inc(s["r_zero"], 1)
            dve.memset(pick3[:], 0.0).then_inc(s["mh_set"], 1)
            dve.memset(epsc[:], EPS).then_inc(s["mh_set"], 1)
            dve.memset(BB[:], 0.0).then_inc(s["mh_set"], 1)
            dve.memset(ones[:], 1.0).then_inc(s["mh_set"], 1)
            dve.memset(zero256[:], 0.0).then_inc(s["mh_set"], 1)
            dve.memset(mean_p[:], 1.0 / P).then_inc(s["mh_set"], 1)
            dve.memset(blk[:], 0.0).then_inc(s["mh_set"], 1)
            dve.wait_ge(s["mh_set"], 7)
            for k in range(3):
                dve.memset(pick3[32 * k:32 * k + 1, :], 1.0).then_inc(s["mh_set"], 1)
            for q in range(Q):
                d = slice(q * C, (q + 1) * C)
                dve.memset(blk[d, d], 1.0 / C).then_inc(s["mh_set"], 1)
            dve.wait_ge(s["ones_set"], 2)
            dve.wait_ge(s["mh_set"], 10 + Q)
            dve.tensor_tensor(cen[:], ident[:], blk[:], ALU.subtract).then_inc(s["consts"], 1)
            dve.wait_ge(s["lnp_in"], 64)
            dve.tensor_copy(lnb[:], lnp[:, 3, 1:2].to_broadcast([P, 96])).then_inc(s["lnb_set"], 1)
            dve.tensor_tensor(ldif[:], lnp[:, 0:3, 1], lnp[:, 0:3, 0], ALU.subtract).then_inc(s["bd_set"], 1)
            dve.wait_ge(s["bd_set"], 1)
            for g in range(3):
                dve.tensor_scalar(blkd[:, g, :], blk[:], ldif[:, g:g + 1], None, ALU.mult).then_inc(s["lnb_set"], 1)
            dve.wait_ge(s["diag_in"], 64)
            dve.tensor_scalar(RS[:, NA], R[:, NA], lnp[:, 3, 0:1], None, ALU.mult).then_inc(s["rs_set"], 1)
            dve.wait_ge(s["braw_in"], 16)
            for n, (a, b, bk, col) in enumerate(BIASES):
                dve.wait_ge(s["bias_mm"], (2, 2, 4, 4, 5)[n])
                prod = bank[bk][0:96 if n == 2 else P, col:col + (b - a) * P]
                if n == 2:
                    dve.tensor_tensor(bsum.rearrange("p (q c) -> p q c", c=C), prod.rearrange("p (q c) -> p q c", c=C),
                                      braw[:].unsqueeze(1).to_broadcast([96, Q, C]), ALU.add).then_inc(s["bsum_set"], 1)
                else:
                    dve.scalar_tensor_tensor(RS[:, a:b], R[:, a:b], lnp[:, NORM[n], 0:1],
                                             prod.rearrange("p (s q c) -> p s q c", q=Q, c=C), ALU.mult, ALU.add)\
                        .then_inc(s["rs_set"], 1)
            for g in range(NZ):
                dve.wait_ge(s["rnz"], g + 1)
                dve.tensor_tensor(Z23[:, g // 8, 4 * (g % 8):4 * (g % 8) + 4, :].rearrange("p i j -> p (i j)"),
                                  bank[cen_bank[g % 6]][:, :], rn[:, g % 2, :], ALU.mult).then_inc(s["zn"], 1)
                if 2 <= g < 10:
                    if g == 2:
                        dve.wait_ge(s["x_in"], 16)
                    for c in range(4 * (g - 2), 4 * (g - 2) + 4):
                        dve.bn_stats(bn[:, c, :], X[:, c, :]).then_inc(s["xbn"], 1)
                if g == 9:
                    dve.wait_ge(s["xbn"], C)
                    row_stats(dve, EPS_C, "xst", 0)
                if g == 12:
                    dve.wait_ge(s["xrs"], 2)
                    dve.scalar_tensor_tensor(st[:, 4, :], st[:, 2, :], -1.0, st[:, 6, :], ALU.mult, ALU.mult)\
                        .then_inc(s["z1_bias"], 1)
                if g >= 12:
                    z1(dve, 4 * (g - 12), 4 * (g - 11), "z1")
                if g == 10:
                    dve.wait_ge(s["bd_in"], 64)
                    dve.wait_ge(s["rs_set"], 5)
                    dve.scalar_tensor_tensor(RS[:, 0:NA], BD[:], 1.0 / C, RS[:, 0:NA], ALU.mult, ALU.add)\
                        .then_inc(s["rs_set"], 1)
                if g == 11:
                    dve.wait_ge(s["mh_set"], 7)
                    dve.wait_ge(s["b_step"], 4)
                    dve.tensor_copy(BB[0:1, :], bhi[0:1, :]).then_inc(s["bb_set"], 1)
                    dve.tensor_copy(BB[32:33, :], bmid[32:33, :]).then_inc(s["bb_set"], 1)
                    dve.tensor_copy(BB[64:65, :], bsum[64:65, :]).then_inc(s["bb_set"], 1)

            def gate(dst, tag, m):
                dve.wait_ge(s["sg" + tag], m + 1)
                dve.tensor_tensor(
                    dst[:].rearrange("p c (q i) -> p i q c", q=Q)[:, 2 * m:2 * m + 2],
                    bank[proj_bank[m % 4]][:, :].rearrange("p (h t q c) -> p h t q c", h=2, t=2, q=Q)[:, :, 0],
                    sg[:, m % 2, :].rearrange("p (h q c) -> p h q c", h=2, q=Q), ALU.mult)\
                    .then_inc(s["gate" + tag], 1)

            for m in range(16):
                gate(p2T, "2", m)
                if m < 2:
                    z1(dve, 16 + m * (Z1_ACT - 16) // 2, 16 + (m + 1) * (Z1_ACT - 16) // 2, "z1")
                if m in (2, 4, 6, 8):
                    k = m // 2 - 1
                    d = slice(k * CH, (k + 1) * CH)
                    dve.wait_ge(s["z1"], Z1_ACT)
                    dve.wait_ge(s["z1a"], C - Z1_ACT)
                    dve.tensor_reduce(mu[:, d], ZA[:, :, d].rearrange("p c j -> p j c"), AX.X, ALU.add)\
                        .then_inc(s["amu"], 1)
                    dve.wait_ge(s["amu"], 2 * k + 1)
                    dve.tensor_scalar(mu[:, d], mu[:, d], 1.0 / C, None, ALU.mult).then_inc(s["amu"], 1)
                if m in (9, 11, 13, 15):
                    k = (m - 9) // 2
                    d = slice(k * CH, (k + 1) * CH)
                    dve.wait_ge(s["asq"], k + 1)
                    dve.tensor_reduce(var[:, d], ZB[:].rearrange("p a b -> p (a b)")[:, k * CH * C:(k + 1) * CH * C]
                                      .rearrange("p (j c) -> p j c", c=C), AX.X, ALU.add).then_inc(s["avar"], 1)
                    dve.wait_ge(s["avar"], 2 * k + 1)
                    dve.tensor_scalar(var[:, d], var[:, d], 1.0 / C, EPS, ALU.mult, ALU.add).then_inc(s["avar"], 1)
            for m in range(16):
                gate(p3T, "3", m)
            for n in range(1, 8, 2):
                dve.wait_ge(s["t1"], n + 1)
                dve.tensor_scalar(ZB[:, 4 * n:4 * n + 4, :].rearrange("p a b -> p (a b)"), bank[1][:, :], 1.0, None, ALU.add)\
                    .then_inc(s["t1d"], 1)
            for n in range(C):
                if n == 2:
                    dve.wait_ge(s["wg_sum"], 1)
                    dve.tensor_tensor(wg_cen[:], wg[:], bank[1][:, 0:E_], ALU.subtract).then_inc(s["wg_set"], 1)
                dve.wait_ge(s["sga"], n + 1)
                dve.tensor_tensor(
                    Z23[:, :, :, 4 * n:4 * n + 4].rearrange("p h c j -> p h j c"),
                    bank[proj_bank[n % 4]][:, :].rearrange("p (h t j c) -> p h t j c", h=2, t=2, c=C)[:, :, 0],
                    sg[:, n % 2, :].rearrange("p (h j c) -> p h j c", h=2, c=C), ALU.mult).then_inc(s["gata"], 1)
            for n in range(1, 8, 2):
                dve.wait_ge(s["tz"], n + 1)
                dve.tensor_copy(ZDf[:, 512 * n:512 * n + 512], bank[1][:, :]).then_inc(s["tzd"], 1)

            def norm5(n):
                dve.wait_ge(s["rn5"], n + 1)
                dve.tensor_tensor(T5[:, 4 * n:4 * n + 4, :].rearrange("p a b -> p (a b)"), bank[1 + n % 3][:, :],
                                  rn[:, n % 2, :], ALU.mult).then_inc(s["norm5"], 1)

            def elu_u(n):
                dve.wait_ge(s["pr5"], n + 1)
                if n >= 2:
                    dve.wait_ge(s["ue5"], n - 1)
                dve.wait_ge(s["g5s"], 8)
                U = sig5[:, 16 * n:16 * n + 16, :].rearrange("p j c -> p (j c)")
                dve.tensor_tensor(U, bank[6 + n % 2][:, :], U, ALU.mult).then_inc(s["u5"], 1)
                dve.wait_ge(s["u5"], n + 1)
                dve.tensor_scalar(um[:, n % 2, :], U, 0.0, None, ALU.min).then_inc(s["um5"], 1)
            for n in range(-1, 10):
                if n + 2 in T5_DVE:
                    dve.wait_ge(s["t5"], n + 3)
                    dve.tensor_copy(T5[:, 4 * (n + 2):4 * (n + 3), :].rearrange("p a b -> p (a b)"), bank[0][:, :])\
                        .then_inc(s["t5d"], 1)
                if 0 <= n < 8:
                    norm5(n)
                if 0 <= n - 1 < 8:
                    elu_u(n - 1)
                if 0 <= n - 2 < 8:
                    elu_add(dve, n - 2)
            x_add(dve, 7)
            dve.wait_ge(s["x2"], 8)
            for c in range(C):
                dve.bn_stats(bn[:, c, :], X[:, c, :]).then_inc(s["tbn"], 1)
            dve.wait_ge(s["tbn"], C)
            row_stats(dve, EPS, "tst", 0)
            dve.wait_ge(s["trs"], 2)
            dve.scalar_tensor_tensor(st[:, 4, :], st[:, 2, :], -1.0, st[:, 6, :], ALU.mult, ALU.mult)\
                .then_inc(s["xl_bias"], 1)
            for c in range(XL_ACT):
                dve.tensor_scalar(XL[:, c, :], X[:, c, :], st[:, 2, c:c + 1], st[:, 6, c:c + 1],
                                  ALU.subtract, ALU.mult).then_inc(s["xln"], 1)
            done = [0]

            def step(ins):
                ins.then_inc(s["rt_"], 1)
                done[0] += 1
                dve.wait_ge(s["rt_"], done[0])

            def ce(k):
                return rt[:, k, :].rearrange("p (c e) -> p c e", e=E_)

            def over_e(v):
                return v.unsqueeze(2).to_broadcast([P, C, E_])

            def over_c(v):
                return v.unsqueeze(1).to_broadcast([P, C, E_])

            dve.wait_ge(s["cst"], 8)
            dve.wait_ge(s["lgt"], 8)
            L = ce(7)
            step(dve.tensor_tensor(L, bank[6][:, 0:256].rearrange("p (c e) -> p c e", e=E_), over_e(st[:, 6, :]),
                                   ALU.mult))
            step(dve.tensor_reduce(rs_[:, 0, :], L, AX.X, ALU.max))
            step(dve.tensor_tensor(ce(0), L, over_e(rs_[:, 0, :]), ALU.subtract))
            dve.wait_ge(s["rex"], 1)
            step(dve.tensor_reduce(rs_[:, 1, :], ce(1), AX.X, ALU.add))
            step(dve.reciprocal(rs_[:, 2, :], rs_[:, 1, :]))
            step(dve.tensor_tensor(ce(2), ce(1), over_e(rs_[:, 2, :]), ALU.mult))
            for k in range(TOP):
                src, hot = ce(2 + k), ce(4 + k)
                step(dve.tensor_reduce(prob[:, k, :], src, AX.X, ALU.max))
                step(dve.tensor_tensor(ce(6), src, over_e(prob[:, k, :]), ALU.is_equal))
                step(dve.tensor_tensor(ce(6), ce(6), over_c(w8[:]), ALU.mult))
                step(dve.tensor_reduce(rs_[:, 3, :], ce(6), AX.X, ALU.max))
                step(dve.tensor_tensor(hot, over_c(w8[:]), over_e(rs_[:, 3, :]), ALU.is_equal))
                if k + 1 < TOP:
                    step(dve.scalar_tensor_tensor(ce(3), hot, -2.0, src, ALU.mult, ALU.add))
            dve.tensor_tensor(M_[:], rt[:, 4, :], rt[:, 5, :], ALU.add).then_inc(s["wk"], 1)
            dve.wait_ge(s["rank"], 1)
            ec = [rt[:, k, :].rearrange("p (e c) -> p e c", c=C) for k in range(12)]
            step(dve.tensor_copy(ec[6], bank[7][:, 256:512].rearrange("p (c e) -> p e c", e=E_)))
            step(dve.tensor_tensor_scan(rt[:, 7, :], rt[:, 6, :], zero256[:], 0.0, ALU.add, ALU.add))
            step(dve.tensor_tensor(rt[:, 8, :], rt[:, 7, :], rt[:, 6, :], ALU.subtract))
            step(dve.tensor_tensor(re_[:, 0, :], ec[7][:, :, C - 1], ec[8][:, :, 0], ALU.subtract))
            step(dve.tensor_tensor(ec[9], re_[:, 0, :].unsqueeze(2).to_broadcast([P, E_, C]),
                                   thr[:].unsqueeze(1).to_broadcast([P, E_, C]), ALU.is_gt))
            step(dve.tensor_reduce(re_[:, 1, :], ec[9], AX.X, ALU.add))
            step(dve.tensor_tensor_scan(re_[:, 2, :], re_[:, 1, :], zero256[:, 0:E_], 0.0, ALU.add, ALU.add))
            step(dve.tensor_tensor(re_[:, 3, :], re_[:, 2, :], re_[:, 1, :], ALU.subtract))
            step(dve.scalar_tensor_tensor(re_[:, 4, :], re_[:, 3, :], float(P), ec[8][:, :, 0], ALU.mult, ALU.subtract))
            step(dve.tensor_tensor(ec[10], ec[8], re_[:, 4, :].unsqueeze(2).to_broadcast([P, E_, C]), ALU.add))
            step(dve.tensor_tensor(ce(11), bank[7][:, 0:256].rearrange("p (c e) -> p c e", e=E_),
                                   rt[:, 10, :].rearrange("p (e c) -> p c e", c=C), ALU.add))
            for k in range(TOP):
                step(dve.tensor_tensor(ce(6), ce(4 + k), ce(11), ALU.mult))
                step(dve.tensor_reduce(slot[:, k, :], ce(6), AX.X, ALU.add))
            step(dve.tensor_copy(sloti[:, 0, :], slot[:].rearrange("p k c -> p (k c)")))
            step(dve.tensor_scalar(sloti[:, 1, :], sloti[:, 0, :], 7, None, ALU.logical_shift_right))
            step(dve.tensor_scalar(sloti[:, 2, :], sloti[:, 0, :], P - 1, None, ALU.bitwise_and))
            step(dve.tensor_copy(slota[:], sloti[:, 1:3, :]))
            n2 = TOP * C

            def same(out, what, count, n):
                return dve.tensor_tensor(out, what.unsqueeze(1).to_broadcast([P, count, n]),
                                         count_r[:, 0:count, 0:n], ALU.is_equal)
            dve.wait_ge(s["count_set"], 1)
            for g in range(PIECES):
                n = slice(g * n2 // PIECES, (g + 1) * n2 // PIECES)
                same(in_tile[:, :, n], slota[:, 0, n], TILES, n2 // PIECES).then_inc(s["vmm"], 1)
                same(BH[:, :, n], slota[:, 1, n], P, n2 // PIECES).then_inc(s["vmm"], 1)
                dve.wait_ge(s["vmm"], 3 * g + 1)
                dve.tensor_tensor(AW[:, 0, :, n], in_tile[:, :, n],
                                  cnum[:, n].unsqueeze(1).to_broadcast([P, TILES, n2 // PIECES]), ALU.mult)\
                    .then_inc(s["vmm"], 1)
            dve.tensor_tensor(te, re_[:, 2, :].unsqueeze(1).to_broadcast([P, ROWS_, E_]),
                              iota_w[:, 0:ROWS_].unsqueeze(2).to_broadcast([P, ROWS_, E_]), ALU.is_le)\
                .then_inc(s["te_set"], 1)
            dve.wait_ge(s["te_set"], 1)
            dve.tensor_reduce(tef[:], te, AX.X, ALU.add).then_inc(s["te_set"], 1)
            dve.wait_ge(s["te_set"], 2)
            dve.tensor_scalar(tile_e[:], tef[:], float(E_ - 1), None, ALU.min).then_inc(s["te_set"], 1)
            dve.wait_ge(s["ve"], 1)
            step(dve.tensor_copy(vt[:, 0, :], bank[0][:, TILES:2 * TILES]))
            step(dve.scalar_tensor_tensor(vt[:, 1, :], bank[0][:, 0:TILES], float(P), vt[:, 0, :], ALU.mult, ALU.add))
            dve.tensor_scalar(vt[:, 5, :], vt[:, 1, :], -float(P), 0.0, ALU.add, ALU.max).then_inc(s["idx_set"], 1)
            dve.scalar_tensor_tensor(vt[:, 2, :], vt[:, 1, :], float(P), spare[:], ALU.is_lt, ALU.mult)\
                .then_inc(s["idx_set"], 1)
            dve.wait_ge(s["idx_set"], 1)
            dve.tensor_scalar(vt[:, 4, :], vt[:, 5, :], float(C * P), -float(C * P), ALU.is_ge, ALU.mult)\
                .then_inc(s["idx_set"], 1)
            dve.wait_ge(s["idx_set"], 2)
            dve.scalar_tensor_tensor(idx[:, 1, :], vt[:, 1, :], -float(P), vt[:, 2, :], ALU.add, ALU.add)\
                .then_inc(s["idx_set"], 1)
            dve.wait_ge(s["idx_set"], 3)
            dve.tensor_tensor(idx[:, 0, :], vt[:, 5, :], vt[:, 4, :], ALU.add).then_inc(s["idx_set"], 1)
            dve.wait_ge(s["idx_set"], 5)
            dve.wait_ge(s["w_in"], 48)

            def gather_index(r, n):
                if not isinstance(r, int) or BODY * r + n >= RING:
                    dve.wait_ge(g_in[n % RING], 16 * (BODY // RING * r + n // RING))
                dve.tensor_copy(gix[:, n % RING, :], idx[:, 0, bass.ds(BODY * r + n, 1)]).then_inc(s["fgi"], 1)

            def scatter_index(r, n):
                if not isinstance(r, int) or BODY * r + n >= RING:
                    dve.wait_ge(sct[n % RING], 16 * (BODY // RING * r + n // RING))
                dve.tensor_copy(six[:, n % RING, :], idx[:, 1, bass.ds(BODY * r + n, 1)]).then_inc(s["fsi"], 1)

            def x_copy(r, n):
                dve.wait_ge(s["ftx"], BODY * r + n + 1)
                past(dve, s["fm1"], r, n - 1)
                dve.tensor_copy(xgT[:, n % 2, :], bank[n % 2][:, 0:P]).then_inc(s["fxc"], 1)

            def add_b1(r, n):
                e = expert_of[n]
                dve.wait_ge(s["fm1"], BODY * r + n + 1)
                past(dve, s["fge"], r, n - 1)
                dve.tensor_tensor(hs[:, n % 2, :].rearrange("p (k t) -> p k t", k=K_),
                                  bank[2 + n % 2][:, :].rearrange("p (k t) -> p k t", k=K_),
                                  b1T[:, bass.ds(e * K_, K_)].unsqueeze(2).to_broadcast([P, K_, P]), ALU.add)\
                    .then_inc(s["fad"], 1)

            def add_b2(r, n):
                e = expert_of[n]
                dve.wait_ge(s["fm2"], BODY * r + n + 1)
                dve.tensor_tensor(ys[:, n % RING, :], bank[6 + n % 2][:, 0:P], b2s[:, bass.ds(e * P, P)], ALU.add)\
                    .then_inc(s["fy"], 1)

            tiles(dve, True, (gather_index, AHEAD), (x_copy, 2), (add_b1, 1), (scatter_index, 0), (add_b2, 0))
            for n, (a, b) in enumerate(PARTS):
                dve.wait_ge(y_in[2 * n], 16)
                for c in range(a, b):
                    dve.scalar_tensor_tensor(X[:, c, :], Y1[:, c, :], prob[:, 0, c:c + 1], X[:, c, :],
                                             ALU.mult, ALU.add).then_inc(s["y_sum"], 1)
                dve.wait_ge(s["y_sum"], b)
                dve.wait_ge(s["y_scaled"], b)
                dve.tensor_tensor(X[:, a:b, :], X[:, a:b, :], Y2[:, a:b, :], ALU.add).then_inc(s["fin"], 1)


def kernel(**inputs):
    import numpy as np
    import concourse.bacc as _bacc
    from concourse.bass_utils import run_bass_kernel_spmd as _run

    c = {k[8:]: np.asarray(v) for k, v in inputs.items() if k.startswith("L0_conv_")}
    names = ["l1", "g1", "l2", "g2", "g5", "l3", "g3", "l4", "g4", "l5"]
    arrays = {
        "x": np.asarray(inputs["x"]), "z2": c["z2"], "z3": c["z3"],
        "conv_w": np.stack([c[n + "_w"] for n in names], axis=1),
        "conv_b": np.stack([c[n + "_b"] for n in names]),
        "ln_p": np.stack([np.stack([c[f"ln{i}_w"], c[f"ln{i}_b"]], axis=1) for i in (1, 2, 3, 5)], axis=1),
    }
    for n in ("W_g", "w1", "b1", "w2", "b2"):
        arrays[n] = np.asarray(inputs["L0_ffn_" + n])
    nc = _bacc.Bacc("TRN2", target_bir_lowering=False, num_devices=1)
    feeds, args = {}, []
    for name, a in arrays.items():
        a = np.ascontiguousarray(a)
        feeds[f"in_{name}"] = a
        args.append(nc.dram_tensor(f"in_{name}", a.shape, mybir.dt.from_np(a.dtype), kind="ExternalInput").ap())
    args.append(nc.dram_tensor("out", (1, C, P, P), F32, kind="ExternalOutput").ap())
    build(nc, *args)
    r = _run(nc, [feeds], core_ids=[0])
    return r.results[0]["out"]
```
